# Optimizing a Trainium2 kernel written in Bass

```python
import numpy as np
import jax
import jax.numpy as jnp

def _softmax(x, axis=-1):
    return jax.nn.softmax(x, axis=axis)

def _gelu(x):
    return jax.nn.gelu(x, approximate=True)

def _silu(x):
    return jax.nn.silu(x)

def _sigmoid(x):
    return jax.nn.sigmoid(x)

def _layernorm(x, axis=-1, eps=1e-05):
    m = jnp.mean(x, axis=axis, keepdims=True)
    v = jnp.var(x, axis=axis, keepdims=True)
    return (x - m) / jnp.sqrt(v + eps)

def _scatter_add(tgt, idx, src, axis=0):
    return tgt.at[idx].add(src)

def _segment_sum(src, seg, n):
    return jax.ops.segment_sum(src, seg, n)
kernel_name = 'mk_xattn_ffn_d1_seqx_r2_3bbf11'

def setup_inputs(seed: int=0):
    np.random.seed(seed)
    _w = jnp.asarray

    def _rec_inputs():
        import jax
        import jax.numpy as jnp
        _rk = jax.random.key(seed)
        x = 7.22e-05 + 1 * jax.random.normal(jax.random.fold_in(_rk, 1), (8, 512, 512), jnp.float32)
        _lenS = 512 - jax.random.randint(jax.random.fold_in(_rk, 7), (8,), 0, max(1, 512 // 4) + 1, jnp.int32)
        _lenS2 = 512 - jax.random.randint(jax.random.fold_in(_rk, 8), (8,), 0, max(1, 512 // 4) + 1, jnp.int32)
        _ctx_1024P = jax.random.normal(jax.random.fold_in(_rk, 11), (8, 16, 512), jnp.float32)
        _ctx_1024c = jax.random.dirichlet(jax.random.fold_in(_rk, 511), 0.3 * jnp.ones((16,), jnp.float32), (8, 512))
        _ctx_1024t = jnp.einsum('bsk,bkd->bsd', _ctx_1024c, _ctx_1024P)
        _ctx_1024t = _ctx_1024t * jax.lax.rsqrt(jnp.mean(jnp.square(_ctx_1024t)) + 1e-12) * 0.953939
        ctx_1024 = 4.13588e-05 + 0.999923 * (_ctx_1024t + 0.3 * jax.random.normal(jax.random.fold_in(_rk, 611), (8, 512, 512), jnp.float32))
        _validS = jnp.arange(512)[None, :] < _lenS[:, None]
        _validS2 = jnp.arange(512)[None, :] < _lenS2[:, None]
        _causal = jnp.tril(jnp.ones((512, 512), dtype=bool))
        mask_BxS2_bf1 = jnp.ones((8, 512), dtype=bool)
        return (x, ctx_1024, mask_BxS2_bf1)
    x, ctx_1024, mask_BxS2_bf1 = _rec_inputs()

    def _L0_xattn_setup():
        import jax, jax.numpy as jnp
        import numpy as np
        N_HEADS = 16
        key = jax.random.key(seed)
        ks = jax.random.split(key, 12)
        b, s, qd, cd, md = (4, 1024, 512, 512, 512)
        inp = {'q': jax.random.normal(ks[0], (b, s, qd), jnp.float32), 'k': jax.random.normal(ks[1], (b, s, cd), jnp.float32), 'v': jax.random.normal(ks[2], (b, s, cd), jnp.float32), 'attention_mask': jnp.ones((b, s), dtype=bool), 'Wq': jax.random.normal(ks[3], (qd, md), jnp.float32) / np.sqrt(qd), 'bq': jnp.zeros((md,), jnp.float32), 'Wk': jax.random.normal(ks[4], (cd, md), jnp.float32) / np.sqrt(cd), 'bk': jnp.zeros((md,), jnp.float32), 'Wv': jax.random.normal(ks[5], (cd, md), jnp.float32) / np.sqrt(cd), 'bv': jnp.zeros((md,), jnp.float32), 'Wo': jax.random.normal(ks[6], (md, qd), jnp.float32) / np.sqrt(md), 'bo': jnp.zeros((qd,), jnp.float32)}
        return inp
    _L0_xattn_all = _L0_xattn_setup()
    _L0_xattn_in = {k: v for k, v in _L0_xattn_all.items() if k in ('Wq', 'bq', 'Wk', 'bk', 'Wv', 'bv', 'Wo', 'bo')}
    del _L0_xattn_all

    def _L0_ffn_setup():
        import jax, jax.numpy as jnp
        import numpy as np
        CAPACITY_FACTOR = 1.0
        key = jax.random.key(seed)
        ks = jax.random.split(key, 5)
        B, S, D, E, F = (2, 1024, 512, 8, 2048)
        x = jax.random.normal(ks[0], (B, S, D), dtype=jnp.float32)
        Ws = jax.random.normal(ks[1], (D, E), dtype=jnp.float32) * (1.0 / np.sqrt(D))
        bs = jnp.zeros((E,), dtype=jnp.float32)
        W1 = jax.random.normal(ks[2], (E, D, F), dtype=jnp.float32) * (1.0 / np.sqrt(D))
        b1 = jnp.zeros((E, F), dtype=jnp.float32)
        W2 = jax.random.normal(ks[3], (E, F, D), dtype=jnp.float32) * (1.0 / np.sqrt(F))
        b2 = jnp.zeros((E, D), dtype=jnp.float32)
        return {'x': x, 'Ws': Ws, 'bs': bs, 'W1': W1, 'b1': b1, 'W2': W2, 'b2': b2}
    _L0_ffn_all = _L0_ffn_setup()
    _L0_ffn_in = {k: v for k, v in _L0_ffn_all.items() if k in ('Ws', 'bs', 'W1', 'b1', 'W2', 'b2')}
    del _L0_ffn_all
    return {'x': x, 'ctx_1024': ctx_1024, 'mask_BxS2_bf1': mask_BxS2_bf1, 'L0_xattn_Wq': _L0_xattn_in['Wq'], 'L0_xattn_bq': _L0_xattn_in['bq'], 'L0_xattn_Wk': _L0_xattn_in['Wk'], 'L0_xattn_bk': _L0_xattn_in['bk'], 'L0_xattn_Wv': _L0_xattn_in['Wv'], 'L0_xattn_bv': _L0_xattn_in['bv'], 'L0_xattn_Wo': _L0_xattn_in['Wo'], 'L0_xattn_bo': _L0_xattn_in['bo'], 'L0_ffn_Ws': _L0_ffn_in['Ws'], 'L0_ffn_bs': _L0_ffn_in['bs'], 'L0_ffn_W1': _L0_ffn_in['W1'], 'L0_ffn_b1': _L0_ffn_in['b1'], 'L0_ffn_W2': _L0_ffn_in['W2'], 'L0_ffn_b2': _L0_ffn_in['b2']}

def reference(x, ctx_1024, mask_BxS2_bf1, L0_xattn_Wq, L0_xattn_bq, L0_xattn_Wk, L0_xattn_bk, L0_xattn_Wv, L0_xattn_bv, L0_xattn_Wo, L0_xattn_bo, L0_ffn_Ws, L0_ffn_bs, L0_ffn_W1, L0_ffn_b1, L0_ffn_W2, L0_ffn_b2):
    import jax
    import jax.numpy as jnp

    def _L0_xattn_ref(q, k, v, attention_mask, Wq, bq, Wk, bk, Wv, bv, Wo, bo):
        import jax, jax.numpy as jnp
        import numpy as np
        N_HEADS = 16
        b, s, _ = q.shape
        n = N_HEADS
        qh = (q @ Wq + bq).reshape(b, s, n, -1).transpose(0, 2, 1, 3)
        kh = (k @ Wk + bk).reshape(b, k.shape[1], n, -1).transpose(0, 2, 1, 3)
        vh = (v @ Wv + bv).reshape(b, v.shape[1], n, -1).transpose(0, 2, 1, 3)
        scale = qh.shape[-1] ** (-0.5)
        sim = jnp.einsum('bnid,bnjd->bnij', qh, kh) * scale
        inv = ~attention_mask
        neg = jnp.finfo(sim.dtype).min
        sim = jnp.where(inv[:, None, None, :], neg, sim)
        attn = jax.nn.softmax(sim, axis=-1)
        out = jnp.einsum('bnij,bnjd->bnid', attn, vh)
        out = out.transpose(0, 2, 1, 3).reshape(b, s, -1)
        return out @ Wo + bo

    def _L0_ffn_ref(x, Ws, bs, W1, b1, W2, b2):
        import jax, jax.numpy as jnp
        import numpy as np
        CAPACITY_FACTOR = 1.0
        B, S, D = x.shape
        E = Ws.shape[1]
        N = B * S
        k = int(CAPACITY_FACTOR * N / E)
        xf = x.reshape(N, D)
        route_prob = jax.nn.softmax(xf @ Ws + bs, axis=-1).T
        route_vals, routes = jax.lax.top_k(route_prob, k)
        xin = xf[routes]
        h = jax.nn.gelu(jnp.einsum('ekd,edf->ekf', xin, W1) + b1[:, None, :])
        out = jnp.einsum('ekf,efd->ekd', h, W2) + b2[:, None, :]
        out = out * route_vals[..., None]
        final = jnp.zeros((N, D), dtype=x.dtype).at[routes.reshape(-1)].add(out.reshape(-1, D))
        return final.reshape(B, S, D)
    x = x + _L0_xattn_ref(_layernorm(x, axis=-1), ctx_1024, ctx_1024, mask_BxS2_bf1, L0_xattn_Wq, L0_xattn_bq, L0_xattn_Wk, L0_xattn_bk, L0_xattn_Wv, L0_xattn_bv, L0_xattn_Wo, L0_xattn_bo)
    x = x + _L0_ffn_ref(_layernorm(x, axis=-1), L0_ffn_Ws, L0_ffn_bs, L0_ffn_W1, L0_ffn_b1, L0_ffn_W2, L0_ffn_b2)
    return x

_drawn_inputs = setup_inputs


def setup_inputs(seed=0):
    import zlib

    import numpy as np

    out = dict(_drawn_inputs(seed))
    spreads = {'L0_xattn_bq': (0.0, 0.1),
     'L0_xattn_bk': (0.0, 0.8),
     'L0_xattn_bv': (0.0, 0.1),
     'L0_xattn_bo': (0.0, 0.1),
     'L0_ffn_bs': (0.0, 0.28),
     'L0_ffn_b1': (0.0, 0.354),
     'L0_ffn_b2': (0.0, 0.1)}
    factors = {}
    for name, (base, spread) in spreads.items():
        noise = np.random.default_rng([zlib.crc32(name.encode()), seed]).standard_normal(out[name].shape)
        drawn = base * np.exp(spread * noise) if base else spread * noise
        out[name] = jnp.asarray(drawn.astype(out[name].dtype))
    for name, factor in factors.items():
        out[name] = (out[name] * factor).astype(out[name].dtype)
    return out
```

```python
from contextlib import ExitStack

import concourse.bass as bass
from concourse import mybir

F32 = mybir.dt.float32
F32R = mybir.dt.float32r
BF16 = mybir.dt.bfloat16
F16 = mybir.dt.float16
I32 = mybir.dt.int32
U8 = mybir.dt.uint8
ALU = mybir.AluOpType
ACT = mybir.ActivationFunctionType
AX = mybir.AxisListType

P = 128
QUAD = 32
BANK = 512
MASKED = 2.0 ** 100


class Sem:

    def __init__(self, ctx, nc, name):
        self.sem = ctx.enter_context(nc.semaphore(name))
        self.count = 0


class Queues:

    def __init__(self):
        self.steps = {"pe": [], "act": [], "dve": [], "pool": [], "sp": []}

    def put(self, engine, waits, run, done=None, by=1):
        if done is not None:
            done.count += by
        self.steps[engine].append((list(waits), run, done, by))
        return None if done is None else (done, done.count)

    def emit(self, engine, handle):
        reached = {}
        for waits, run, done, by in self.steps[engine]:
            for sem, value in waits:
                if reached.get(id(sem), 0) < value:
                    handle.wait_ge(sem.sem, value)
                    reached[id(sem)] = value
            last = run(handle)
            if done is not None:
                last.then_inc(done.sem, by)


def attention_moe_kernel(nc, x, ctx_in, mask, Wq, bq, Wk, bk, Wv, bv, Wo, bo,
                         Ws, bs, W1, b1, W2, b2, out, hn_rows, mask_rows):
    B, S, D = x.shape
    SK = ctx_in.shape[1]
    E = Ws.shape[1]
    F = W1.shape[2]
    DH = QUAD
    H = D // DH
    N = B * S
    K = N // E
    DC = D // P
    TB = S // P
    KT = SK // P
    NT = N // P
    HG = P // DH
    GB = H // HG
    NG = B * GB
    SCALE = float(DH) ** -0.5
    EPS = 1e-5
    ROW = hn_rows.shape[1]
    assert S == SK == D == K == BANK and E == 8 and H == 16 and P == 8 * 16

    x_tok = x.rearrange("b s d -> (b s) d")
    ctx_tok = ctx_in.rearrange("b s d -> (b s) d")
    out_tok = out.rearrange("b s d -> (b s) d")
    q = Queues()
    put = q.put

    with ExitStack() as top:
        def sem(name):
            return Sem(top, nc, name)

        def sb(scope, name, shape, dt=F32):
            return scope.enter_context(nc.sbuf_tensor(name, shape, dt))

        NSC = 3
        ps_sc = [top.enter_context(nc.psum_tensor(f"ps_sc{i}", [P, BANK], F32)) for i in range(NSC)]
        ps_att = top.enter_context(nc.psum_tensor("ps_att", [P, BANK], F32))
        ps_den = top.enter_context(nc.psum_tensor("ps_den", [P, BANK], F32))
        ps_gen = [top.enter_context(nc.psum_tensor(f"ps_gen{i}", [P, BANK], F32)) for i in range(3)]

        ident = sb(top, "ident", [P, P])
        probs = sb(top, "probs", [P, NT, E])
        b1_cols = sb(top, "b1_cols", [P, P])
        s_const = sem("s_const")
        s_bias_in = sem("s_bias_in")

        put("pool", [], lambda e: e.memset(ident[:, :], 0.0), s_const)
        t_zero = (s_const, s_const.count)
        t_ident = put("pool", [t_zero], lambda e: e.affine_select(
            out=ident[:, :], in_=ident[:, :], compare_op=ALU.not_equal, fill=1.0, base=0,
            pattern=[[-1, P]], channel_multiplier=1), s_const)

        ROW_BANK = 2
        gen_free = [[], [], []]
        gen_turn = [1]
        gen_open = set()

        def take_bank(i=None):
            if i is None:
                gen_turn[0] += 1
                if gen_turn[0] % 2 in gen_open:
                    gen_turn[0] += 1
                i = gen_turn[0] % 2
            waits, gen_free[i] = gen_free[i], []
            return i, waits

        s_gen = sem("s_gen")
        s_ev_act = sem("s_ev_act")
        s_ev_dve = sem("s_ev_dve")

        def raw(ap):
            return ap.bitcast(F32)

        def three(psum, pairs, e):
            n = len(pairs)
            for i, ((wh, wl), (mh, ml)) in enumerate(pairs):
                e.matmul(psum, lhsT=wh, rhs=mh, start=(i == 0), stop=False)
                e.matmul(psum, lhsT=wh, rhs=ml, start=False, stop=False)
                last = e.matmul(psum, lhsT=wl, rhs=mh, start=False, stop=(i == n - 1))
            return last

        s_hn_store = [sem(f"s_hn_store{i}") for i in range(2)]
        s_probs_store = sem("s_probs_store")
        s_x1_store = [sem(f"s_x1_store{i}") for i in range(2)]
        t_x1_all, t_hn_all = [], []

        with ExitStack() as p1:
            w_hi = {w: sb(p1, f"w{w}_hi", [P, DC, D], F32R) for w in "qkvo"}
            w_lo = {w: sb(p1, f"w{w}_lo", [P, DC, D], F32R) for w in "qkvo"}
            ws_sb = sb(p1, "ws_sb", [P, DC, E])
            bs_b = sb(p1, "bs_b", [P, E])
            bo_b = sb(p1, "bo_b", [P, D])
            ones = sb(p1, "ones", [P, QUAD])
            bias_cols = sb(p1, "bias_cols", [P, 3 * DC])
            half = sb(p1, "half", [P, 1])
            keep_scale = sb(p1, "keep_scale", [P, B])
            NH_ = 1
            xT = [sb(p1, f"xT_{k}", [P, DC, S], F32R) for k in ("hi", "lo")]
            cT = [sb(p1, f"cT_{k}", [P, DC, SK], F32R) for k in ("hi", "lo")]
            qk = {(w, k): sb(p1, f"{w}T_{k}", [P, S], F32R) for w in "qk" for k in ("hi", "lo")}
            NST = 3
            kst = [sb(p1, f"kst{i}", [P, HG, SK], F32R) for i in range(NST)]
            qst = [sb(p1, f"qst{i}", [P, HG, S], F32R) for i in range(NST)]
            ROW_MASK, ROWS_MAX, ROWS_ALL = 3 * DH, 3 * DH + 1, 3 * DH + 3
            v_sb = sb(p1, "v_sb", [P, KT, D])
            NP_ = 6
            p_ring = [sb(p1, f"p_ring{i}", [P, S]) for i in range(NP_)]
            NX = 3
            x_in = [sb(p1, f"x_in{i}", [P, D]) for i in range(NX)]
            maxes = sb(p1, "maxes", [P, HG * TB])
            nmax = [sb(p1, f"nmax_{k}", [HG * TB, P], F32R) for k in ("hi", "lo")]
            rden = sb(p1, "rden", [P, S])
            oT = [sb(p1, f"oT_{k}", [P, GB, S], F32R) for k in ("hi", "lo")]
            x1 = sb(p1, "x1", [P, D])
            hn = [sb(p1, f"hn{i}", [P, D]) for i in range(NH_)]
            hnT = sb(p1, "hnT", [P, DC, P])
            stat = [sb(p1, f"stat{i}", [P, 6]) for i in range(2)]
            mv = [sb(p1, f"mv{i}", [P, 2]) for i in range(2)]
            rstd = [sb(p1, f"rstd{i}", [P, 1]) for i in range(2)]
            rt_max = sb(p1, "rt_max", [P, TB])
            rt_sum = sb(p1, "rt_sum", [P, TB])

            ones_b = hnT[0:B, 0, :]
            mask_u8 = hnT[0:B, 1, :].bitcast(U8)
            bias_rows = hnT[0:3 * DC, 2, :]
            mask_neg = rden[0:B, :]

            put("pool", [], lambda e: e.memset(ones[:, :], 1.0), s_const)
            put("pool", [], lambda e: e.memset(half[:, :], -0.5), s_const)
            for i in range(NST):
                put("pool", [(s_const, s_const.count)], lambda e, i=i: e.memset(raw(kst[i][ROW_MASK:P, :, :]), 1.0), s_const)
                put("pool", [(s_const, s_const.count)], lambda e, i=i: e.memset(raw(qst[i][ROW_MASK:P, :, :]), 1.0), s_const)
            t_const = (s_const, s_const.count)

            put("sp", [], lambda e: e.dma_start(ws_sb[:, :, :], Ws.rearrange("(c p) n -> p c n", p=P)), s_bias_in, 16)
            put("sp", [], lambda e: e.dma_start(bs_b[:, :], bs.rearrange("(a n) -> a n", a=1).to_broadcast([P, E])), s_bias_in, 16)
            put("sp", [], lambda e: e.dma_start(bo_b[:, :], bo.rearrange("(a n) -> a n", a=1).to_broadcast([P, D])), s_bias_in, 16)
            for n, v in enumerate((bq, bk, bv)):
                put("sp", [], lambda e, n=n, v=v: e.dma_start(
                    bias_rows[n * DC:(n + 1) * DC, :], v.rearrange("(c p) -> c p", p=P)), s_bias_in, 16)
            put("sp", [], lambda e: e.dma_start(mask_u8, mask), s_bias_in, 16)
            t_bias_in = (s_bias_in, s_bias_in.count)

            s_mask = sem("s_mask")
            t = put("dve", [t_bias_in], lambda e: e.tensor_scalar(
                mask_neg, mask_u8, 1.0, MASKED, ALU.subtract, ALU.mult), s_mask)
            s_mask_store = sem("s_mask_store")
            t_mask = put("sp", [t], lambda e: e.dma_start(raw(mask_rows), mask_neg), s_mask_store, 16)

            s_w_in = [sem(f"s_w_in{i}") for i in range(NP_)]
            s_w_hi, s_w_lo = sem("s_w_hi"), sem("s_w_lo")
            stage_free = [[] for _ in range(NP_)]
            t_w = {}
            n = 0
            for w, src in (("q", Wq), ("k", Wk), ("v", Wv), ("o", Wo)):
                for c in range(DC):
                    slot, n = n % NP_, n + 1
                    t_in = put("sp", stage_free[slot], lambda e, s=slot, c=c, src=src: e.dma_start(
                        p_ring[s][:, :], src[c * P:(c + 1) * P, :]),
                        s_w_in[slot], 16)
                    t_hi = put("act", [t_in], lambda e, s=slot, c=c, w=w: e.activation(
                        w_hi[w][:, c, :], p_ring[s][:, :], ACT.Copy), s_w_hi)
                    t_lo = put("dve", [t_in, t_hi], lambda e, s=slot, c=c, w=w: e.tensor_tensor(
                        w_lo[w][:, c, :], p_ring[s][:, :], raw(w_hi[w][:, c, :]), ALU.subtract), s_w_lo)
                    stage_free[slot] = [t_hi, t_lo]
                t_w[w] = [t_hi, t_lo]

            mask_any = sb(p1, "mask_any", [B, 1])
            mask_diag = sb(p1, "mask_diag", [B, B])
            s_any = sem("s_any")
            t_ones_b = put("dve", [], lambda e: e.memset(ones_b, SCALE), s_any)
            t_any = put("dve", [t_bias_in], lambda e: e.reduce_max(mask_any[:, :], mask_u8, AX.X), s_any)
            t_any = put("dve", [t_any, t_ident], lambda e: e.tensor_scalar(
                mask_diag[:, :], ident[0:B, 0:B], mask_any[:, 0:1], None, ALU.mult), s_any)
            bank, free = take_bank()
            t = put("pe", free + [t_any, t_ones_b], lambda e, bank=bank: e.matmul(
                ps_gen[bank][:, 0:B], lhsT=ones_b, rhs=mask_diag[:, :], start=True, stop=True), s_gen)
            t_keep = put("dve", [t], lambda e, bank=bank: e.tensor_copy(keep_scale[:, :], ps_gen[bank][:, 0:B]), s_ev_dve)
            gen_free[bank] = [t_keep]
            bank, free = take_bank()
            t = put("pe", free + [t_bias_in, t_ident], lambda e, bank=bank: e.transpose(
                ps_gen[bank][:, 0:3 * DC], bias_rows, ident[0:3 * DC, 0:3 * DC]), s_gen)
            t_bias = put("dve", [t], lambda e, bank=bank: e.tensor_copy(bias_cols[:, :], ps_gen[bank][:, 0:3 * DC]), s_ev_dve)
            gen_free[bank] = [t_bias]

            x_in_free = [[] for _ in range(NX)]
            s_x_in = [sem(f"s_x_in{i}") for i in range(NX)]
            x_turn = [0]
            t_xT_read, t_cT_read = [], []
            s_ln = sem("s_ln")
            s_rs = sem("s_rs")
            s_norm = sem("s_norm")
            ln_turn = [0]
            ln_free = [[], []]

            def layernorm(src, dst, t_src, dst_free):
                i = ln_turn[0] % 2
                ln_turn[0] += 1
                t = put("dve", t_src + ln_free[i], lambda e: e.bn_stats(stat[i][:, :], src), s_ln)
                t_mv = put("dve", [t], lambda e: e.bn_aggr(mv[i][:, :], stat[i][:, :]), s_ln)
                t = put("dve", [t_mv], lambda e: e.tensor_scalar(rstd[i][:, :], mv[i][:, 1:2], EPS, None, ALU.add), s_ln)
                t = put("pool", [t, t_const], lambda e: e.tensor_tensor(rstd[i][:, :], rstd[i][:, :], half[:, :], ALU.pow), s_rs)
                t = put("dve", [t] + dst_free, lambda e: e.tensor_scalar(
                    dst, src, mv[i][:, 0:1], rstd[i][:, 0:1], ALU.subtract, ALU.mult), s_norm)
                ln_free[i] = [t]
                return t

            def store_split(bank, dst, view, bias, t_full, waits):
                if bias is None:
                    t_hi = put("act", [t_full] + waits, lambda e: e.activation(dst[0], view, ACT.Copy), s_ev_act)
                    t_lo = put("dve", [t_full, t_hi] + waits, lambda e: e.tensor_tensor(
                        dst[1], view, raw(dst[0]), ALU.subtract), s_ev_dve)
                else:
                    t_hi = put("act", [t_full, t_bias] + waits, lambda e: e.activation(
                        dst[0], view, ACT.Identity, bias=bias), s_ev_act)
                    t_lo = put("dve", [t_full, t_hi] + waits, lambda e: e.scalar_tensor_tensor(
                        dst[1], view, bias, raw(dst[0]), ALU.add, ALU.subtract), s_ev_dve)
                gen_free[bank] = [t_hi, t_lo]
                return [t_hi, t_lo]

            t_tr = {}
            loaded = {}

            def load_tile(kind, b, t):
                slot = x_turn[0] % NX
                x_turn[0] += 1
                src = (x_tok if kind == "x" else ctx_tok)[(b * TB + t) * P:(b * TB + t + 1) * P, :]
                tk = put("sp", x_in_free[slot], lambda e: e.dma_start(x_in[slot][:, :], src), s_x_in[slot], 16)
                if kind == "x":
                    tk = layernorm(x_in[slot][:, :], x_in[slot][:, :], [tk], [])
                loaded[kind, b, t] = (slot, tk)

            def transpose_tile(kind, b, t):
                slot, tk = loaded[kind, b, t]
                dst = xT if kind == "x" else cT
                bank, free = take_bank()

                def run(e):
                    for c in range(DC):
                        last = e.transpose(ps_gen[bank][:, c * P:(c + 1) * P], x_in[slot][:, c * P:(c + 1) * P], ident[:, :])
                    return last
                tf = put("pe", free + [tk, t_ident], run, s_gen)
                x_in_free[slot] = [tf]
                view = ps_gen[bank][:, :].rearrange("p (c t) -> p c t", c=DC)
                cols = [d[:, :, t * P:(t + 1) * P] for d in dst]
                old = t_xT_read if kind == "x" else t_cT_read
                t_tr.setdefault((kind, b), []).extend(store_split(bank, cols, view, None, tf, list(old)))

            v_free = []
            t_v = {}

            def project_v(b, t):
                bank, free = take_bank()
                cols = slice(t * P, (t + 1) * P)

                tf = put("pe", free + t_tr["c", b] + t_w["v"], lambda e: three(
                    ps_gen[bank][:, :], [((cT[0][:, c, cols], cT[1][:, c, cols]),
                                          (w_hi["v"][:, c, :], w_lo["v"][:, c, :])) for c in range(DC)], e), s_gen)
                t_cT_read[:] = [tf]
                tv = put("act", [tf] + v_free, lambda e: e.activation(v_sb[:, t, :], ps_gen[bank][:, :], ACT.Copy), s_ev_act)
                gen_free[bank] = [tv]
                t_v[b] = tv

            s_stack = [{w: sem(f"s_stack_{w}{i}") for w in "qk"} for i in range(NST)]
            s_mask_row = [sem(f"s_mask_row{i}") for i in range(NST)]
            stack_free = [[] for _ in range(NST)]
            t_stack = {}
            qk_free = {"q": [], "k": []}

            def project_qk(w, g):
                b, c4 = divmod(g, GB)
                k = g % NST
                src = xT if w == "q" else cT
                dst = qst[k] if w == "q" else kst[k]
                cols = slice(c4 * P, (c4 + 1) * P)
                held = {}

                def begin():
                    held["bank"], free = take_bank()
                    gen_open.add(held["bank"])
                    return free

                def finish(tf):
                    bank = held["bank"]
                    gen_open.discard(bank)
                    (t_xT_read if w == "q" else t_cT_read)[:] = [tf]
                    n = ("q", "k").index(w) * DC + c4
                    parts = store_split(bank, [qk[w, "hi"][:, :], qk[w, "lo"][:, :]], ps_gen[bank][:, :],
                                        bias_cols[:, n:n + 1], tf, qk_free[w])
                    order = ("hi", "lo", "hi") if w == "q" else ("hi", "hi", "lo")
                    sm = s_stack[k][w]
                    for part in ("hi", "lo"):
                        for h in range(HG):
                            for r in range(3):
                                if order[r] != part:
                                    continue
                                put("sp", [parts[("hi", "lo").index(part)], t_const] + stack_free[k],
                                    lambda e, h=h, r=r, part=part: e.dma_start(
                                        raw(dst[r * DH:(r + 1) * DH, h, :]), raw(qk[w, part][h * DH:(h + 1) * DH, :])), sm, 16)
                    qk_free[w] = [(sm, sm.count)]
                    if w == "k":
                        src_m = raw(mask_rows[b:b + 1, :]).rearrange("p (a n) -> p a n", a=1).to_broadcast([1, HG, SK])
                        t_stack["mask", g] = put("sp", [t_mask], lambda e: e.dma_start(
                            raw(kst[k][ROW_MASK:ROW_MASK + 1, :, :]), src_m), s_mask_row[k], 16)
                    t_stack[w, g] = (sm, sm.count)

                def part(i):
                    free = begin() if i == 0 else []
                    wh, wl = w_hi[w][:, i, cols], w_lo[w][:, i, cols]
                    mh, ml = src[0][:, i, :], src[1][:, i, :]
                    psum = ps_gen[held["bank"]][:, :]

                    def run(e):
                        e.matmul(psum, lhsT=wh, rhs=mh, start=(i == 0), stop=False)
                        e.matmul(psum, lhsT=wh, rhs=ml, start=False, stop=False)
                        return e.matmul(psum, lhsT=wl, rhs=mh, start=False, stop=(i == DC - 1))
                    waits = free + t_tr["x" if w == "q" else "c", b] + t_w[w] if i == 0 else []
                    tf = put("pe", waits, run, s_gen)
                    if i == DC - 1:
                        finish(tf)
                return [lambda i=i: part(i) for i in range(DC)]

            s_max = sem("s_max")
            s_maxrow = [sem(f"s_maxrow{i}") for i in range(NST)]
            t_maxrow = {}
            maxes_free, nmax_free = [], []
            last_max = [None]

            def row_max(g, h, t):
                bank, free = take_bank(ROW_BANK)
                ks, qs = kst[g % NST], qst[g % NST]
                tf = put("pe", free + [t_stack["q", g], t_stack["k", g], t_stack["mask", g]], lambda e: e.matmul(
                    ps_gen[bank][:, :], lhsT=qs[0:ROWS_MAX, h, t * P:(t + 1) * P], rhs=ks[0:ROWS_MAX, h, :],
                    start=True, stop=True), s_gen)
                col = h * TB + t
                tm = put("dve", [tf] + maxes_free, lambda e: e.reduce_max(maxes[:, col:col + 1], ps_gen[bank][:, :], AX.X), s_max)
                gen_free[bank] = [tm]
                last_max[0] = (tf, tm)

            def max_rows(g):
                tf, tm = last_max[0]
                bank, free = take_bank()
                tt = put("pe", free + [tm, t_ident], lambda e: e.transpose(
                    ps_gen[bank][0:HG * TB, 0:P], maxes[:, :], ident[:, :]), s_gen)
                maxes_free[:] = [tt]
                view = ps_gen[bank][0:HG * TB, 0:P]
                t_hi = put("act", [tt] + nmax_free, lambda e: e.activation(nmax[0][:, :], view, ACT.Copy, scale=-1.0), s_ev_act)
                t_lo = put("dve", [tt, t_hi] + nmax_free, lambda e: e.scalar_tensor_tensor(
                    nmax[1][:, :], view, -1.0, raw(nmax[0][:, :]), ALU.mult, ALU.subtract), s_ev_dve)
                gen_free[bank] = [t_hi, t_lo]
                sm = s_maxrow[g % NST]
                for r in range(2):
                    row = ROWS_MAX + r
                    dst = qst[g % NST][row:row + 1, :, :].rearrange("p h (t n) -> p (h t) n", n=P)
                    put("sp", [t_hi, t_lo, tf], lambda e, r=r, dst=dst: e.dma_start(raw(dst), raw(nmax[r][:, :])), sm, 16)
                nmax_free[:] = [(sm, sm.count)]
                t_maxrow[g] = (sm, sm.count)

            s_st, s_exp, s_av = sem("s_st"), sem("s_exp"), sem("s_av")
            sc_free = [[] for _ in range(NSC)]
            p_free = [[] for _ in range(NP_)]
            p_slot = {}
            sc_turn = [0]

            def scores(g, kt, h):
                ks, qs = kst[g % NST], qst[g % NST]
                k, slot = sc_turn[0] % NSC, sc_turn[0] % NP_
                sc_turn[0] += 1
                ts = put("pe", sc_free[k] + [t_maxrow[g]], lambda e: e.matmul(
                    ps_sc[k][:, :], lhsT=ks[0:ROWS_ALL, h, kt * P:(kt + 1) * P], rhs=qs[0:ROWS_ALL, h, :],
                    start=True, stop=True), s_st)
                if kt == KT - 1:
                    stack_free[g % NST] = [ts]
                b = g // GB
                te = put("act", [ts, t_keep] + p_free[slot], lambda e: e.activation(
                    p_ring[slot][:, :], ps_sc[k][:, :], ACT.Exp, scale=keep_scale[:, b:b + 1]), s_exp)
                sc_free[k] = [te]
                p_slot[g, kt, h] = (slot, te)

            att_free = []
            t_oT = {}
            oT_free = []
            s_nrm, s_oh, s_ol = sem("s_nrm"), sem("s_oh"), sem("s_ol")
            nrm_free = [t_mask, t_bias, t_keep]

            def attend(g, kt, psum):
                b, c4 = divmod(g, GB)
                slots = [p_slot[g, kt, h] for h in range(HG)]

                def run(e):
                    for h in range(HG):
                        w = v_sb[:, kt, (c4 * HG + h) * DH:(c4 * HG + h + 1) * DH] if psum is ps_att else ones[:, :]
                        last = e.matmul(psum[h * DH:(h + 1) * DH, :], lhsT=w, rhs=p_ring[slots[h][0]][:, :],
                                        start=(kt == 0), stop=(kt == KT - 1))
                    return last
                ta = put("pe", [s[1] for s in slots] + [t_v[b], t_const] + (list(att_free) if kt == 0 else []), run, s_av)
                for s in slots:
                    p_free[s[0]] = [ta]
                if psum is ps_att:
                    return
                if kt < KT - 1:
                    return
                if c4 == GB - 1:
                    v_free[:] = [ta]
                t = put("dve", [ta] + nrm_free, lambda e: e.reciprocal(rden[:, :], ps_den[:, :]), s_nrm)
                tn = put("dve", [t], lambda e: e.tensor_tensor(rden[:, :], ps_att[:, :], rden[:, :], ALU.mult), s_nrm)
                att_free[:] = [tn]
                bias = bias_cols[:, 2 * DC + c4:2 * DC + c4 + 1]
                th = put("act", [tn, t_bias] + oT_free, lambda e: e.activation(
                    oT[0][:, c4, :], rden[:, :], ACT.Identity, bias=bias), s_oh)
                tl = put("dve", [tn, th] + oT_free, lambda e: e.scalar_tensor_tensor(
                    oT[1][:, c4, :], rden[:, :], bias, raw(oT[0][:, c4, :]), ALU.add, ALU.subtract), s_ol)
                nrm_free[:] = [th, tl]
                t_oT[b] = [th, tl]

            s_x1 = sem("s_x1")
            x1_free = []
            hn_free = [[] for _ in range(NH_)]
            t_hn = {}

            def output_tile(b, t):
                n = b * TB + t
                rows = slice(n * P, (n + 1) * P)
                xs = x_turn[0] % NX
                x_turn[0] += 1
                xres = x_in[xs]
                tr = put("sp", x_in_free[xs], lambda e: e.dma_start(xres[:, :], x_tok[rows, :]), s_x_in[xs], 16)
                tr = put("pool", [tr, t_bias_in], lambda e: e.tensor_tensor(xres[:, :], xres[:, :], bo_b[:, :], ALU.add), s_x1)
                bank, free = take_bank()
                cols = slice(t * P, (t + 1) * P)
                tf = put("pe", free + t_oT[b] + t_w["o"], lambda e: three(
                    ps_gen[bank][:, :], [((oT[0][:, c, cols], oT[1][:, c, cols]),
                                          (w_hi["o"][:, c, :], w_lo["o"][:, c, :])) for c in range(GB)], e), s_gen)
                oT_free[:] = [tf]
                t1 = put("dve", [tf, tr] + x1_free, lambda e: e.tensor_tensor(
                    x1[:, :], ps_gen[bank][:, :], xres[:, :], ALU.add), s_ev_dve)
                gen_free[bank] = [t1]
                x_in_free[xs] = [t1]
                sm = s_x1_store[0]
                ts = put("sp", [t1], lambda e: e.dma_start(out_tok[rows, :], x1[:, :]), sm, 16)
                slot = n % NH_
                th = layernorm(x1[:, :], hn[slot][:, :], [t1], hn_free[slot])
                x1_free[:] = [ts, th]
                sh = s_hn_store[slot]
                tsh = put("sp", [th], lambda e: e.dma_start(hn_rows[rows, 0:D], hn[slot][:, :]), sh, 16)
                t_hn[n] = (slot, th, tsh)

            s_hnT, s_lg = sem("s_hnT"), sem("s_lg")
            hnT_free = []

            def route_tile(b, t):
                n = b * TB + t
                slot, th, tsh = t_hn[n]
                bank, free = take_bank()

                def run(e):
                    for c in range(DC):
                        last = e.transpose(ps_gen[bank][:, c * P:(c + 1) * P], hn[slot][:, c * P:(c + 1) * P], ident[:, :])
                    return last
                tf = put("pe", free + [th], run, s_gen)
                hn_free[slot] = [tf, tsh]
                tc = put("act", [tf] + hnT_free, lambda e: e.activation(
                    hnT[:, :, :], ps_gen[bank][:, :].rearrange("p (c t) -> p c t", c=DC), ACT.Copy), s_ev_act)
                gen_free[bank] = [tc]
                bank2, free2 = take_bank()

                def run2(e):
                    for c in range(DC):
                        last = e.matmul(ps_gen[bank2][:, 0:E], lhsT=hnT[:, c, :], rhs=ws_sb[:, c, :], start=(c == 0), stop=(c == DC - 1))
                    return last
                tf2 = put("pe", free2 + [tc, t_bias_in], run2, s_gen)
                hnT_free[:] = [tf2]
                tl = put("dve", [tf2], lambda e: e.tensor_tensor(probs[:, n, :], ps_gen[bank2][:, 0:E], bs_b[:, :], ALU.add), s_ev_dve)
                gen_free[bank2] = [tl]
                if t == TB - 1:
                    softmax_rows(b, tl)

            def softmax_rows(b, t):
                v = probs[:, b * TB:(b + 1) * TB, :]
                def wide(a):
                    return a[:, :].rearrange("p (t a) -> p t a", a=1).to_broadcast([P, TB, E])
                t = put("dve", [t], lambda e: e.reduce_max(rt_max[:, :], v, AX.X), s_lg)
                t = put("dve", [t], lambda e: e.tensor_tensor(v, v, wide(rt_max), ALU.subtract), s_lg)
                t = put("act", [t], lambda e: e.activation(v, v, ACT.Exp), s_hnT)
                t = put("dve", [t], lambda e: e.reduce_sum(rt_sum[:, :], v, AX.X), s_lg)
                t = put("dve", [t], lambda e: e.reciprocal(rt_sum[:, :], rt_sum[:, :]), s_lg)
                t = put("dve", [t], lambda e: e.tensor_tensor(v, v, wide(rt_sum), ALU.mult), s_lg)
                rows = hn_rows[b * S:(b + 1) * S, D:D + E].rearrange("(t p) e -> p t e", p=P)
                put("sp", [t], lambda e: e.dma_start(rows, v), s_probs_store, 16)
                return t

            def prepare(b):
                order = [("c", t) for t in range(TB)] + [("x", t) for t in range(TB)]
                todo = list(order)
                for _ in range(2):
                    load_tile(todo[0][0], b, todo.pop(0)[1])
                items = []
                for k, t in order:
                    def item(k=k, t=t):
                        if todo:
                            load_tile(todo[0][0], b, todo.pop(0)[1])
                        transpose_tile(k, b, t)
                    items.append(item)
                return items

            def spread_out(first, second):
                n = [(k / max(1, len(first)), 0, k) for k in range(len(first))]
                n += [(k / max(1, len(second)), 1, k) for k in range(len(second))]
                return [(first, second)[which][k] for _, which, k in sorted(n)]

            def maxes_of(g):
                if not 0 <= g < NG:
                    return []
                return [lambda h=h, t=t: row_max(g, h, t) for h in range(HG) for t in range(TB)] + [lambda: max_rows(g)]

            def projections(g):
                if g >= NG:
                    return []
                first = prepare(g // GB) if g % GB == 0 else []
                return first + project_qk("k", g) + project_qk("q", g)

            def late(b):
                return [f for t in range(TB) for f in (lambda t=t: output_tile(b, t), lambda t=t: route_tile(b, t))]

            def around(i):
                rest = projections(i + 2)
                if i >= GB and i % GB == 0:
                    tail = late(i // GB - 1)
                    rest = rest[:4] + spread_out(tail, rest[4:])
                rows_ = maxes_of(i + 1)
                head = spread_out(rows_, rest[:-2])
                return head + rest[-2:]

            for item in projections(0) + projections(1) + maxes_of(0):
                item()
            GAPS = 5 * KT
            for i in range(NG):
                items = around(i)
                done, gap = [0], [0]

                def fill():
                    gap[0] += 1
                    upto = len(items) * gap[0] // GAPS
                    while done[0] < upto:
                        items[done[0]]()
                        done[0] += 1
                    if i % GB == 0 and 3 <= gap[0] < 3 + KT:
                        project_v(i // GB, gap[0] - 3)
                for kt in range(KT):
                    before = (i, kt - 1) if kt else (i - 1, KT - 1)
                    scores(i, kt, 0)
                    scores(i, kt, 1)
                    fill()
                    if before[0] >= 0:
                        attend(*before, ps_att)
                    fill()
                    if before[0] >= 0:
                        attend(*before, ps_den)
                    scores(i, kt, 2)
                    fill()
                    scores(i, kt, 3)
                    fill()
                    fill()
            attend(NG - 1, KT - 1, ps_att)
            attend(NG - 1, KT - 1, ps_den)
            for item in late(B - 1):
                item()
            t_probs = (s_lg, s_lg.count)
            t_x1_all = [(s, s.count) for s in s_x1_store]
            t_hn_all = [(s, s.count) for s in s_hn_store + [s_probs_store]]
            t_part1 = [(s, s.count) for s in (s_gen, s_st, s_av, s_ev_act, s_ev_dve, s_exp, s_oh, s_ol, s_nrm,
                                              s_norm, s_hnT, s_lg, s_x1)] + t_x1_all + t_hn_all

        gate_stack = top
        idx = sb(gate_stack, "idx", [P, E, K // P], I32)
        HALF = E // 2
        A_N, B_N = QUAD, K // QUAD
        with ExitStack() as p2:
            s_go = sem("s_go")
            pT = sb(p2, "pT", [P, 2 * P])
            expert_of = sb(p2, "expert_of", [P, E])
            same = sb(p2, "same", [P, P], BF16)
            tri = sb(p2, "tri", [P, P], BF16)
            ones_h = sb(p2, "ones_h", [P, P], BF16)
            ones_f = sb(p2, "ones_f", [P, P])
            junk = sb(p2, "junk", [P, 2 * P], BF16)
            cnt = sb(p2, "cnt", [P, 1], F32)
            cnt_h = sb(p2, "cnt_h", [P, 1], BF16)
            thr = sb(p2, "thr", [P, 1], I32)
            cand = sb(p2, "cand", [P, 1], I32)
            okc = sb(p2, "okc", [P, 1])
            thr_d = sb(p2, "thr_d", [P, E])
            thr_b = sb(p2, "thr_b", [P, E])
            marks = sb(p2, "marks", [P, 2, NT, E], BF16)
            tot = [sb(p2, f"tot{i}", [P, 2, NT, E]) for i in range(2)]
            first = sb(p2, "first", [P, 2, NT, E])
            slot_f = sb(p2, "slot_f", [P, NT, E])
            slot_e = sb(p2, "slot_e", [P, NT, E])
            slot_i = sb(p2, "slot_i", [P, NT, E], I32)
            sa = sb(p2, "sa", [P, NT, E], I32)
            sbb = sb(p2, "sbb", [P, NT, E], I32)
            sa_h = sb(p2, "sa_h", [P, NT, E], F16)
            sb_h = sb(p2, "sb_h", [P, NT, E], F16)
            iota = sb(p2, "iota", [P, QUAD], F16)
            tok = sb(p2, "tok", [P, NT], F16)
            hot_a = sb(p2, "hot_a", [P, NT * E, A_N], F16)
            hot_b = sb(p2, "hot_b", [P, NT * E, B_N], F16)
            s_c2, s_sel, s_cnt, s_tot2 = sem("s_c2"), sem("s_sel"), sem("s_cnt"), sem("s_tot2")

            def dve(waits, run):
                return put("dve", waits, run, s_sel)

            TOK0 = N // 2
            put("pool", t_part1, lambda e: e.iota(iota[:, :], pattern=[[1, QUAD]], base=0, channel_multiplier=0,
                                                  allow_small_or_imprecise_dtypes=True), s_c2)
            put("pool", [(s_c2, s_c2.count)], lambda e: e.iota(tok[:, :], pattern=[[P, NT]], base=-TOK0, channel_multiplier=1,
                                             allow_small_or_imprecise_dtypes=True), s_c2)
            put("pool", [(s_c2, s_c2.count)], lambda e: e.memset(ones_h[:, :], 1.0), s_c2)
            put("pool", [(s_c2, s_c2.count)], lambda e: e.memset(ones_f[:, :], 1.0), s_c2)
            t = (s_c2, s_c2.count)
            put("pool", [t], lambda e: e.affine_select(out=tri[:, :], in_=ones_h[:, :], compare_op=ALU.is_ge, fill=0.0,
                                                       base=0, pattern=[[1, P]], channel_multiplier=-1), s_c2)
            t_c2 = (s_c2, s_c2.count)
            t = dve(t_part1, lambda e: e.reduce_max(expert_of[:, :], ident[:, :].rearrange("p (t e) -> p e t", e=E), AX.X))
            t_same = dve([t], lambda e: e.tensor_copy(
                same[:, :].rearrange("p (t e) -> p t e", e=E),
                expert_of[:, :].rearrange("p (a e) -> p a e", a=1).to_broadcast([P, P // E, E])))
            t_thr0 = dve([], lambda e: e.memset(thr[:, :], 0))

            bank, free = take_bank()

            def run(e):
                for r in range(2):
                    last = e.transpose(ps_gen[bank][:, r * P:(r + 1) * P],
                                       probs[:, r * 16:(r + 1) * 16, :].rearrange("p t e -> p (t e)"), ident[:, :])
                return last
            t = put("pe", free + t_part1, run, s_gen)
            t_pT = dve([t], lambda e: e.tensor_copy(pT[:, :], ps_gen[bank][:, 0:2 * P]))

            t_thr = t_thr0
            for bit in range(29, -1, -1):
                t = dve([t_thr], lambda e, bit=bit: e.tensor_single_scalar(cand[:, :], thr[:, :], 1 << bit, ALU.bitwise_or))
                t = dve([t, t_pT], lambda e: e.tensor_scalar(
                    junk[:, :], pT[:, :], cand[:, 0:1].bitcast(F32), 0.0, ALU.is_ge, ALU.add, accum_out=cnt[:, :]))
                t = dve([t], lambda e: e.tensor_copy(cnt_h[:, :], cnt[:, :]))
                t = put("pe", [t, t_same], lambda e: e.matmul(ps_den[:, 0:1], lhsT=same[:, :], rhs=cnt_h[:, :], start=True, stop=True), s_cnt)
                t = dve([t], lambda e: e.scalar_tensor_tensor(
                    okc[:, :], ps_den[:, 0:1], float(K), cand[:, :].bitcast(F32), ALU.is_ge, ALU.mult))
                t_thr = dve([t], lambda e: e.tensor_tensor(thr[:, :].bitcast(F32), thr[:, :].bitcast(F32), okc[:, :], ALU.max))

            t = dve([t_thr], lambda e: e.tensor_scalar(thr_d[:, :], ident[:, 0:E], thr[:, 0:1].bitcast(F32), None, ALU.mult))
            t = put("pe", [t, t_c2], lambda e: e.matmul(ps_den[:, 0:E], lhsT=ones_f[:, :], rhs=thr_d[:, :], start=True, stop=True), s_cnt)
            t = dve([t], lambda e: e.tensor_copy(thr_b[:, :], ps_den[:, 0:E]))
            wide_thr = thr_b[:, :].rearrange("p (a e) -> p a e", a=1).to_broadcast([P, NT, E])
            dve([t], lambda e: e.tensor_tensor(marks[:, 0, :, :], probs[:, :, :], wide_thr, ALU.is_gt))
            t_marks = dve([], lambda e: e.tensor_tensor(marks[:, 1, :, :], probs[:, :, :], wide_thr, ALU.is_equal))
            flat = marks[:, :, :, :].rearrange("p m t e -> p (m t e)")
            t_in = put("pe", [t_marks, t_c2], lambda e: e.matmul(ps_att[:, :], lhsT=tri[:, :], rhs=flat, start=True, stop=True), s_tot2)
            t_tt = put("pe", [], lambda e: e.matmul(ps_den[:, :], lhsT=ones_h[:, :], rhs=flat, start=True, stop=True), s_tot2)
            merged = "p m t e -> p (m t e)"
            t = dve([t_tt], lambda e: e.tensor_copy(tot[0][:, :, :, :].rearrange(merged), ps_den[:, :]))
            t_first = dve([t], lambda e: e.tensor_copy(first[:, :, :, :], tot[0][:, :, :, :]))
            t = t_first
            step, cur = 1, 0
            while step < NT:
                a, b_ = tot[cur], tot[1 - cur]
                dve([t], lambda e, a=a, b_=b_, s=step: e.tensor_copy(b_[:, :, 0:s, :], a[:, :, 0:s, :]))
                t = dve([], lambda e, a=a, b_=b_, s=step: e.tensor_tensor(
                    b_[:, :, s:NT, :], a[:, :, s:NT, :], a[:, :, 0:NT - s, :], ALU.add))
                step, cur = 2 * step, 1 - cur
            run_tot, rank = tot[cur], tot[1 - cur]
            t = dve([t], lambda e: e.tensor_tensor(first[:, :, :, :], run_tot[:, :, :, :], first[:, :, :, :], ALU.subtract))
            t = dve([t, t_in], lambda e: e.tensor_tensor(rank[:, :, :, :].rearrange(merged), ps_att[:, :], first[:, :, :, :].rearrange(merged), ALU.add))
            above = run_tot[:, 0, NT - 1:NT, :].to_broadcast([P, NT, E])
            t = dve([t], lambda e: e.tensor_tensor(slot_e[:, :, :], rank[:, 1, :, :], above, ALU.add))
            t = dve([t], lambda e: e.tensor_tensor(slot_e[:, :, :], slot_e[:, :, :], marks[:, 1, :, :], ALU.mult))
            t = dve([t], lambda e: e.tensor_tensor(slot_f[:, :, :], rank[:, 0, :, :], marks[:, 0, :, :], ALU.mult))
            t = dve([t], lambda e: e.tensor_tensor(slot_f[:, :, :], slot_f[:, :, :], slot_e[:, :, :], ALU.add))
            t = dve([t], lambda e: e.tensor_scalar(slot_i[:, :, :], slot_f[:, :, :], -1.0, None, ALU.add))
            dve([t], lambda e: e.tensor_single_scalar(sa[:, :, :], slot_i[:, :, :], A_N - 1, ALU.bitwise_and))
            t = dve([], lambda e: e.tensor_single_scalar(sbb[:, :, :], slot_i[:, :, :], 5, ALU.arith_shift_right))
            dve([t], lambda e: e.tensor_copy(sa_h[:, :, :], sa[:, :, :]))
            t = dve([], lambda e: e.tensor_copy(sb_h[:, :, :], sbb[:, :, :]))

            def spread(a, n):
                return a[:, :, :].rearrange("p t e -> p (t e)").rearrange("p (c a) -> p c a", a=1).to_broadcast([P, NT * E, n])

            def count(n):
                return iota[:, 0:n].rearrange("p (a n) -> p a n", a=1).to_broadcast([P, NT * E, n])
            t_b = dve([t, t_c2], lambda e: e.tensor_tensor(hot_b[:, :, :], spread(sb_h, B_N), count(B_N), ALU.is_equal))
            view = hot_b[:, :, :].rearrange("p (t e) b -> p t (e b)", e=E)
            t_b = dve([t_b], lambda e: e.tensor_tensor(
                view, view, tok[:, :].rearrange("p (t a) -> p t a", a=1).to_broadcast([P, NT, E * B_N]), ALU.mult))
            t_a = dve([], lambda e: e.tensor_tensor(hot_a[:, :, :], spread(sa_h, A_N), count(A_N), ALU.is_equal))
            t_idx = None
            for hf in range(2):
                psum = ps_gen[hf]

                def run(e, hf=hf, psum=psum):
                    for n in range(NT):
                        c = slice(n * E + hf * HALF, n * E + (hf + 1) * HALF)
                        last = e.matmul(psum[:, 0:HALF * B_N], lhsT=hot_a[:, c, :].rearrange("p e a -> p (e a)"),
                                        rhs=hot_b[:, c, :].rearrange("p e b -> p (e b)"), start=(n == 0), stop=(n == NT - 1))
                    return last
                t = put("pe", [t_a, t_b, t_pT], run, s_cnt)
                for e4 in range(HALF):
                    for r in range(P // QUAD):
                        srcv = psum[e4 * QUAD:(e4 + 1) * QUAD, e4 * B_N + r:(e4 + 1) * B_N:P // QUAD]
                        t_idx = dve([t], lambda e, srcv=srcv, r=r, k=hf * HALF + e4: e.tensor_scalar(
                            idx[r * QUAD:(r + 1) * QUAD, k, :], srcv, float(TOK0), None, ALU.add))

        FB = 2 * P
        NPIECE = F // FB
        NF = F // P
        TT = K // P
        with ExitStack() as p3:
            NR, NS = 3, 3
            w1_raw = [sb(p3, f"w1_raw{i}", [P, DC, FB]) for i in range(NR)]
            w2_raw = [sb(p3, f"w2_raw{i}", [P, 2, D]) for i in range(NR)]
            w1s = [[sb(p3, f"w1_{k}{i}", [P, DC, FB], F32R) for k in ("hi", "lo")] for i in range(NS)]
            w2s = [[sb(p3, f"w2_{k}{i}", [P, 2, D], F32R) for k in ("hi", "lo")] for i in range(NS)]
            rows = [sb(p3, f"rows{i}", [P, ROW]) for i in range(2 * TT)]
            hT = [[sb(p3, f"hT_{k}{i}", [P, DC, K], F32R) for k in ("hi", "lo")] for i in range(2)]
            gel = [sb(p3, f"gel{i}", [P, K]) for i in range(2)]
            gel_s = [[sb(p3, f"gel_{k}{i}", [P, K], F32R) for k in ("hi", "lo")] for i in range(2)]
            b2_b = [sb(p3, f"b2_b{i}", [P, D]) for i in range(2)]
            y_sb = [sb(p3, f"y_sb{i}", [P, D]) for i in range(TT)]
            y_out = [sb(p3, f"y_out{i}", [P, D]) for i in range(TT)]
            b1_raw = sb(p3, "b1_raw", [P, P])

            t_part2 = [t_idx, (s_cnt, s_cnt.count), (s_tot2, s_tot2.count), t_c2]
            s_w1_in = [sem(f"s_w1_in{i}") for i in range(NR)]
            s_w2_in = [sem(f"s_w2_in{i}") for i in range(NR)]
            s_b1, s_b2 = sem("s_b1"), [sem(f"s_b2{i}") for i in range(2)]
            s_split = sem("s_split")
            s_rows = [sem(f"s_rows{i}") for i in range(2 * TT)]
            s_up, s_gelu, s_gel_lo, s_down = sem("s_up"), sem("s_gelu"), sem("s_gel_lo"), sem("s_down")
            s_yb, s_y, s_add = sem("s_yb"), sem("s_y"), [sem(f"s_add{i}") for i in range(TT)]
            ps_up = ps_gen
            ps_y = [p[:, :] for p in (*ps_sc, ps_gen[ROW_BANK])]
            ps_tr = [ps_att, ps_den]
            up_free, tr_free = [[], []], [[], []]
            y_free = [[] for _ in range(TT)]

            t_b1in = put("sp", t_part2 + t_part1, lambda e: e.dma_start(b1_raw[:, :], b1.rearrange("e (j p) -> (e j) p", p=P)), s_b1, 16)
            t = put("pe", [t_b1in] + t_part2, lambda e: e.transpose(ps_att[:, 0:P], b1_raw[:, :], ident[:, :]), s_gen)
            t_b1 = put("dve", [t], lambda e: e.tensor_copy(b1_cols[:, :], ps_att[:, 0:P]), s_ev_dve)
            tr_free[0] = [t_b1]

            raw_free = [[] for _ in range(NR)]
            split_free = [[[], []] for _ in range(NS)]
            pieces = [(e, j) for e in range(E) for j in range(NPIECE)]
            t_in, t_sp = {}, {}

            def load_piece(n):
                ex, j = pieces[n]
                r = n % NR
                w1v = W1[ex, :, j * FB:(j + 1) * FB].rearrange("(c p) f -> p c f", p=P)
                w2v = W2[ex, j * FB:(j + 1) * FB, :].rearrange("(c p) d -> p c d", p=P)
                ta = put("sp", raw_free[r], lambda e: e.dma_start(w1_raw[r][:, :, :], w1v), s_w1_in[r], 16)
                tb = put("sp", raw_free[r], lambda e: e.dma_start(w2_raw[r][:, :, :], w2v), s_w2_in[r], 16)
                t_in[n] = (ta, tb)

            def split_piece(n):
                r, s = n % NR, n % NS
                got = []
                for k, (rw, sp_) in enumerate(((w1_raw[r], w1s[s]), (w2_raw[r], w2s[s]))):
                    th = put("dve", [t_in[n][k]] + split_free[s][k] + t_part2, lambda e, rw=rw, sp_=sp_: e.tensor_copy(
                        sp_[0][:, :, :], rw[:, :, :]), s_split)
                    tl = put("dve", [th], lambda e, rw=rw, sp_=sp_: e.tensor_tensor(
                        sp_[1][:, :, :], rw[:, :, :], raw(sp_[0][:, :, :]), ALU.subtract), s_split)
                    got.append(tl)
                raw_free[r] = [tl]
                t_sp[n] = got

            rows_free = [[] for _ in range(2 * TT)]
            t_rows = {}

            def gather(ex):
                for tt in range(TT):
                    slot = (ex % 2) * TT + tt
                    t_rows[ex, tt] = put("pool", rows_free[slot] + [t_idx] + t_hn_all + t_part2, lambda e, slot=slot, tt=tt: e.indirect_dma_start(
                        rows[slot][:, :], None, hn_rows[:, :], bass.IndirectOffsetOnAxis(ap=idx[:, ex, tt:tt + 1], axis=0)), s_rows[slot], 16)

            hT_free = [[], []]
            t_hT = {}

            def transpose_rows(ex, tt):
                slot = (ex % 2) * TT + tt
                k = tt % 2
                psum = ps_tr[k]

                def run(e):
                    for c in range(DC):
                        last = e.transpose(psum[:, c * P:(c + 1) * P], rows[slot][:, c * P:(c + 1) * P], ident[:, :])
                    return last
                tf = put("pe", tr_free[k] + [t_rows[ex, tt]] + t_part2, run, s_gen)
                view = psum[:, :].rearrange("p (c t) -> p c t", c=DC)
                dst = [d[:, :, tt * P:(tt + 1) * P] for d in hT[ex % 2]]
                th = put("act", [tf] + hT_free[ex % 2], lambda e: e.activation(dst[0], view, ACT.Copy), s_ev_act)
                tl = put("dve", [tf, th] + hT_free[ex % 2], lambda e: e.tensor_tensor(dst[1], view, raw(dst[0]), ALU.subtract), s_ev_dve)
                tr_free[k] = [th, tl]
                t_hT[ex] = [th, tl]

            s_gfree = [[], []]
            t_gel = {}

            def up(ex, j):
                n = ex * NPIECE + j // 2
                w = w1s[n % NS]
                col = slice((j % 2) * P, (j % 2 + 1) * P)
                k = j % 2
                hh = hT[ex % 2]
                tf = put("pe", up_free[k] + [t_sp[n][0]] + t_hT[ex], lambda e: three(
                    ps_up[k][:, :], [((w[0][:, c, col], w[1][:, c, col]), (hh[0][:, c, :], hh[1][:, c, :])) for c in range(DC)], e), s_up)
                if j % 2:
                    split_free[n % NS][0] = [tf]
                if j == NF - 1:
                    hT_free[ex % 2] = [tf]
                bias = b1_cols[:, ex * NF + j:ex * NF + j + 1]
                tg = put("act", [tf, t_b1] + s_gfree[k], lambda e: e.activation(
                    gel[k][:, :], ps_up[k][:, :], ACT.Gelu_apprx_tanh, bias=bias), s_gelu)
                th = put("act", [tf, t_b1] + s_gfree[k], lambda e: e.activation(
                    gel_s[k][0][:, :], ps_up[k][:, :], ACT.Gelu_apprx_tanh, bias=bias), s_gelu)
                up_free[k] = [th]
                tl = put("dve", [th], lambda e: e.tensor_tensor(
                    gel_s[k][1][:, :], gel[k][:, :], raw(gel_s[k][0][:, :]), ALU.subtract), s_gel_lo)
                t_gel[ex, j] = [th, tl]

            def down(ex, j):
                n = ex * NPIECE + j // 2
                w = w2s[n % NS]
                k = j % 2

                def run(e):
                    for tt in range(TT):
                        c = slice(tt * P, (tt + 1) * P)
                        gh, gl = gel_s[k][0][:, c], gel_s[k][1][:, c]
                        wh, wl = w[0][:, j % 2, :], w[1][:, j % 2, :]
                        e.matmul(ps_y[tt], lhsT=gh, rhs=wh, start=(j == 0), stop=False)
                        e.matmul(ps_y[tt], lhsT=gh, rhs=wl, start=False, stop=False)
                        last = e.matmul(ps_y[tt], lhsT=gl, rhs=wh, start=False, stop=(j == NF - 1))
                    return last
                waits = [w for f in y_free for w in f] if j == 0 else []
                tf = put("pe", waits + t_gel[ex, j] + [t_sp[n][1]], run, s_down)
                s_gfree[k] = [tf]
                if j % 2:
                    split_free[n % NS][1] = [tf]
                return tf

            b2_free = [[], []]
            y_sb_free = [[] for _ in range(TT)]
            y_out_free = [[] for _ in range(TT)]
            t_b2 = {}

            def load_b2(ex):
                k = ex % 2
                t_b2[ex] = put("sp", b2_free[k] + t_part2 + t_part1, lambda e: e.dma_start(
                    b2_b[k][:, :], b2[ex:ex + 1, :].to_broadcast([P, D])), s_b2[k], 16)

            t_added = [list(t_x1_all)]

            def finish(ex, tf):
                k = ex % 2
                before = t_added[0]
                mine = []
                for tt in range(TT):
                    slot = k * TT + tt
                    ty = put("dve", [tf, t_b2[ex]] + y_sb_free[tt], lambda e, tt=tt: e.tensor_tensor(
                        y_sb[tt][:, :], ps_y[tt], b2_b[k][:, :], ALU.add), s_yb)
                    y_free[tt] = [ty]
                    to = put("act", [ty] + y_out_free[tt], lambda e, tt=tt, slot=slot: e.activation(
                        y_out[tt][:, :], y_sb[tt][:, :], ACT.Copy, scale=rows[slot][:, D + ex:D + ex + 1]), s_y)
                    y_sb_free[tt] = [to]
                    rows_free[slot] = [to]
                    ta = put("pool", [to] + before, lambda e, tt=tt: e.indirect_dma_start(
                        out_tok, bass.IndirectOffsetOnAxis(ap=idx[:, ex, tt:tt + 1], axis=0),
                        y_out[tt][:, :], None, compute_op=ALU.add), s_add[tt], 16)
                    y_out_free[tt] = [ta]
                    mine.append(ta)
                b2_free[k] = [ty]
                t_added[0] = mine

            for n in range(NR):
                if n == 0:
                    q.steps["sp"].append(([*t_part1, *t_part2], lambda e: None, None, 0))
                load_piece(n)
            gather(0)
            load_b2(0)
            split_piece(0)
            for tt in range(TT):
                transpose_rows(0, tt)
            split_piece(1)
            gather(1)
            load_b2(1)
            order = [(ex, j) for ex in range(E) for j in range(NF)]
            up(0, 0)
            for i, (ex, j) in enumerate(order):
                if i + 1 < len(order):
                    up(*order[i + 1])
                tf = down(ex, j)
                if j % 2 == 1:
                    n = i // 2
                    if n + NR < len(pieces):
                        load_piece(n + NR)
                    if n + 2 < len(pieces):
                        split_piece(n + 2)
                if ex + 1 < E and NF - 6 <= j < NF - 2:
                    transpose_rows(ex + 1, j - (NF - 6))
                if j == NF - 1:
                    finish(ex, tf)
                    if ex + 2 < E:
                        gather(ex + 2)
                        load_b2(ex + 2)
            q.steps["pool"].append((t_added[0], lambda e: None, None, 0))

        with nc.Block() as block:
            @block.sync
            def _(e):
                q.emit("sp", e)

            @block.gpsimd
            def _(e):
                q.emit("pool", e)

            @block.scalar
            def _(e):
                q.emit("act", e)

            @block.vector
            def _(e):
                q.emit("dve", e)

            @block.tensor
            def _(e):
                q.emit("pe", e)


_INS = ['x', 'ctx_1024', 'mask_BxS2_bf1', 'L0_xattn_Wq', 'L0_xattn_bq', 'L0_xattn_Wk', 'L0_xattn_bk', 'L0_xattn_Wv',
        'L0_xattn_bv', 'L0_xattn_Wo', 'L0_xattn_bo', 'L0_ffn_Ws', 'L0_ffn_bs', 'L0_ffn_W1', 'L0_ffn_b1', 'L0_ffn_W2',
        'L0_ffn_b2']


def kernel(**inputs):
    import numpy as np
    import concourse.bacc as bacc
    from concourse.bass_utils import run_bass_kernel_spmd

    nc = bacc.Bacc("TRN2", target_bir_lowering=False, num_devices=1)
    arrays, args = {}, []
    for name in _INS:
        a = np.ascontiguousarray(inputs[name])
        arrays[f"in_{name}"] = a
        args.append(nc.dram_tensor(f"in_{name}", a.shape, mybir.dt.from_np(a.dtype), kind="ExternalInput").ap())
    b, s, d = inputs['x'].shape
    e = inputs['L0_ffn_Ws'].shape[1]
    out = nc.dram_tensor("out_x", (b, s, d), F32, kind="ExternalOutput").ap()
    hn_rows = nc.dram_tensor("hn_rows", (b * s, d + e), F32, kind="Internal").ap()
    mask_rows = nc.dram_tensor("mask_rows", inputs['mask_BxS2_bf1'].shape, F32R, kind="Internal").ap()
    attention_moe_kernel(nc, *args, out, hn_rows, mask_rows)
    r = run_bass_kernel_spmd(nc, [arrays], core_ids=[0])
    return r.results[0]["out_x"]
```

```python
from contextlib import ExitStack

import concourse.bass as bass
from concourse import mybir

F32 = mybir.dt.float32
F32R = mybir.dt.float32r
BF16 = mybir.dt.bfloat16
F16 = mybir.dt.float16
I32 = mybir.dt.int32
U8 = mybir.dt.uint8
ALU = mybir.AluOpType
ACT = mybir.ActivationFunctionType
AX = mybir.AxisListType

P = 128
QUAD = 32
BANK = 512
MASKED = 2.0 ** 100


class Sem:

    def __init__(self, ctx, nc, name):
        self.sem = ctx.enter_context(nc.semaphore(name))
        self.count = 0


class Queues:

    def __init__(self):
        self.steps = {"pe": [], "act": [], "dve": [], "pool": [], "sp": []}

    def put(self, engine, waits, run, done=None, by=1):
        if done is not None:
            done.count += by
        self.steps[engine].append((list(waits), run, done, by))
        return None if done is None else (done, done.count)

    def emit(self, engine, handle):
        reached = {}
        for waits, run, done, by in self.steps[engine]:
            for sem, value in waits:
                if reached.get(id(sem), 0) < value:
                    handle.wait_ge(sem.sem, value)
                    reached[id(sem)] = value
            last = run(handle)
            if done is not None:
                last.then_inc(done.sem, by)


def attention_moe_kernel(nc, x, ctx_in, mask, Wq, bq, Wk, bk, Wv, bv, Wo, bo,
                         Ws, bs, W1, b1, W2, b2, out, hn_rows, mask_rows):
    B, S, D = x.shape
    SK = ctx_in.shape[1]
    E = Ws.shape[1]
    F = W1.shape[2]
    DH = QUAD
    H = D // DH
    N = B * S
    K = N // E
    DC = D // P
    TB = S // P
    KT = SK // P
    NT = N // P
    HG = P // DH
    GB = H // HG
    NG = B * GB
    SCALE = float(DH) ** -0.5
    EPS = 1e-5
    ROW = hn_rows.shape[1]
    assert S == SK == D == K == BANK and E == 8 and H == 16 and P == 8 * 16

    x_tok = x.rearrange("b s d -> (b s) d")
    ctx_tok = ctx_in.rearrange("b s d -> (b s) d")
    out_tok = out.rearrange("b s d -> (b s) d")
    q = Queues()
    put = q.put

    with ExitStack() as top:
        def sem(name):
            return Sem(top, nc, name)

        def sb(scope, name, shape, dt=F32):
            return scope.enter_context(nc.sbuf_tensor(name, shape, dt))

        NGEN = 6
        ps_att = top.enter_context(nc.psum_tensor("ps_att", [P, BANK], F32))
        ps_den = top.enter_context(nc.psum_tensor("ps_den", [P, BANK], F32))
        ps_gen = [top.enter_context(nc.psum_tensor(f"ps_gen{i}", [P, BANK], F32)) for i in range(NGEN)]

        ident = sb(top, "ident", [P, P])
        probs = sb(top, "probs", [P, NT, E])
        s_const = sem("s_const")
        s_bias_in = sem("s_bias_in")

        put("pool", [], lambda e: e.memset(ident[:, :], 0.0), s_const)
        t_zero = (s_const, s_const.count)
        t_ident = put("pool", [t_zero], lambda e: e.affine_select(
            out=ident[:, :], in_=ident[:, :], compare_op=ALU.not_equal, fill=1.0, base=0,
            pattern=[[-1, P]], channel_multiplier=1), s_const)

        gen_free = [[] for _ in range(NGEN)]
        gen_order = list(range(NGEN))
        deferred = []

        def flush():
            while deferred:
                deferred.pop(0)()
        gen_open = set()
        gen_late = set()

        def take_bank():
            i = next(k for k in gen_order if k not in gen_open)
            gen_order.remove(i)
            gen_order.append(i)
            if i in gen_late:
                flush()
            waits, gen_free[i] = gen_free[i], []
            return i, waits

        s_gen = sem("s_gen")
        s_ev_act = sem("s_ev_act")
        s_ev_dve = sem("s_ev_dve")

        def raw(ap):
            return ap.bitcast(F32)

        def three(psum, pairs, e):
            n = len(pairs)
            for i, ((wh, wl), (mh, ml)) in enumerate(pairs):
                e.matmul(psum, lhsT=wh, rhs=mh, start=(i == 0), stop=False)
                e.matmul(psum, lhsT=wh, rhs=ml, start=False, stop=False)
                last = e.matmul(psum, lhsT=wl, rhs=mh, start=False, stop=(i == n - 1))
            return last

        s_hn_store = sem("s_hn_store")
        s_probs_store = sem("s_probs_store")
        s_x1_store = sem("s_x1_store")
        t_x1_all, t_hn_all = [], []

        with ExitStack() as p1:
            w_hi = {w: sb(p1, f"w{w}_hi", [P, DC, D], F32R) for w in "qkvo"}
            w_lo = {w: sb(p1, f"w{w}_lo", [P, DC, D], F32R) for w in "qkvo"}
            ws_sb = sb(p1, "ws_sb", [P, DC, QUAD])
            bs_b = sb(p1, "bs_b", [P, E])
            bo_b = sb(p1, "bo_b", [P, D])
            ones = sb(p1, "ones", [P, QUAD])
            bias_cols = sb(p1, "bias_cols", [P, 3 * DC])
            half = sb(p1, "half", [P, 1])
            keep_scale = sb(p1, "keep_scale", [P, B])
            xT = [sb(p1, f"xT_{k}", [P, DC, S], F32R) for k in ("hi", "lo")]
            cT = [sb(p1, f"cT_{k}", [P, DC, SK], F32R) for k in ("hi", "lo")]
            qk = {(w, k): sb(p1, f"{w}T_{k}", [P, S], F32R) for w in "qk" for k in ("hi", "lo")}
            NST = 3
            kst = [sb(p1, f"kst{i}", [P, HG, SK], F32R) for i in range(NST)]
            qst = [sb(p1, f"qst{i}", [P, HG, S], F32R) for i in range(NST)]
            ROW_MASK, ROWS_MAX, ROWS_ALL = 3 * DH, 3 * DH + 1, 3 * DH + 3
            v_sb = sb(p1, "v_sb", [P, KT, D])
            NP_ = 6
            p_ring = [sb(p1, f"p_ring{i}", [P, S]) for i in range(NP_)]
            NX = 4
            x_in = [sb(p1, f"x_in{i}", [P, D]) for i in range(NX)]
            maxes = sb(p1, "maxes", [P, HG * TB])
            nmax = [sb(p1, f"nmax_{k}", [HG * TB, P], F32R) for k in ("hi", "lo")]
            rden = sb(p1, "rden", [P, S])
            att_n = sb(p1, "att_n", [P, S])
            oT = [sb(p1, f"oT_{k}", [P, GB, S], F32R) for k in ("hi", "lo")]
            hnT = sb(p1, "hnT", [P, DC, P])
            stat = [sb(p1, f"stat{i}", [P, 6]) for i in range(2)]
            mv = [sb(p1, f"mv{i}", [P, 2]) for i in range(2)]
            rstd = [sb(p1, f"rstd{i}", [P, 1]) for i in range(2)]
            rt_max = sb(p1, "rt_max", [P, TB])
            rt_sum = sb(p1, "rt_sum", [P, TB])

            ones_b = hnT[0:B, 0, :]
            mask_u8 = hnT[0:B, 1, :].bitcast(U8)
            bias_rows = hnT[0:3 * DC, 2, :]
            mask_neg = rden[0:B, :]

            x_in_free = [[] for _ in range(NX)]
            s_x_in = [sem(f"s_x_in{i}") for i in range(NX)]
            x_turn = [0]
            t_xT_read, t_cT_read = [], []
            s_ln = sem("s_ln")
            s_rs = sem("s_rs")
            s_norm = sem("s_norm")
            ln_turn = [0]
            ln_free = [[], []]

            def layernorm(src, dst, t_src, dst_free, then):
                i = ln_turn[0] % 2
                ln_turn[0] += 1
                t = put("dve", t_src + ln_free[i], lambda e: e.bn_stats(stat[i][:, :], src), s_ln)
                t_mv = put("dve", [t], lambda e: e.bn_aggr(mv[i][:, :], stat[i][:, :]), s_ln)
                t = put("dve", [t_mv], lambda e: e.tensor_scalar(rstd[i][:, :], mv[i][:, 1:2], EPS, None, ALU.add), s_ln)
                t = put("pool", [t, t_ws0], lambda e: e.tensor_tensor(rstd[i][:, :], rstd[i][:, :], half[:, :], ALU.pow), s_rs)

                def normalise():
                    tn = put("dve", [t] + dst_free(), lambda e: e.tensor_scalar(
                        dst, src, mv[i][:, 0:1], rstd[i][:, 0:1], ALU.subtract, ALU.mult), s_norm)
                    ln_free[i] = [tn]
                    then(tn)
                deferred.append(normalise)

            def store_split(bank, dst, view, bias, t_full, waits, stored, lo_waits=()):
                if bias is None:
                    t_hi = put("act", [t_full] + waits, lambda e: e.activation(dst[0], view, ACT.Copy), s_ev_act)
                else:
                    t_hi = put("act", [t_full, t_bias] + waits, lambda e: e.activation(
                        dst[0], view, ACT.Identity, bias=bias), s_ev_act)

                def lo():
                    w = [t_full, t_hi, *lo_waits] + waits
                    if bias is None:
                        t_lo = put("dve", w, lambda e: e.tensor_tensor(dst[1], view, raw(dst[0]), ALU.subtract), s_ev_dve)
                    else:
                        t_lo = put("dve", w, lambda e: e.scalar_tensor_tensor(
                            dst[1], view, bias, raw(dst[0]), ALU.add, ALU.subtract), s_ev_dve)
                    gen_free[bank] = [t_hi, t_lo]
                    gen_late.discard(bank)
                    stored(t_hi, t_lo)
                gen_late.add(bank)
                deferred.append(lo)

            t_tr = {}
            loaded = {}

            s_first_in = [sem(f"s_first_in{i}") for i in range(NX)]

            def load_tile(kind, b, t):
                engine, sems = ("sp", s_first_in) if b == 0 else ("pool", s_x_in)
                slot = x_turn[0] % NX
                x_turn[0] += 1
                src = (x_tok if kind == "x" else ctx_tok)[(b * TB + t) * P:(b * TB + t + 1) * P, :]
                tk = put(engine, x_in_free[slot], lambda e: e.dma_start(x_in[slot][:, :], src), sems[slot], 16)
                loaded[kind, b, t] = (slot, tk)

            def normalise_tile(b, t):
                slot, tk = loaded["x", b, t]
                layernorm(x_in[slot][:, :], x_in[slot][:, :], [tk], lambda: [],
                          lambda tn: loaded.update({("x", b, t): (slot, tn)}))

            def transpose_tile(kind, b, t):
                slot, tk = loaded[kind, b, t]
                dst = xT if kind == "x" else cT
                bank, free = take_bank()

                def run(e):
                    for c in range(DC):
                        last = e.transpose(ps_gen[bank][:, c * P:(c + 1) * P], x_in[slot][:, c * P:(c + 1) * P], ident[:, :])
                    return last
                tf = put("pe", free + [tk, t_ident], run, s_gen)
                x_in_free[slot] = [tf]
                view = ps_gen[bank][:, :].rearrange("p (c t) -> p c t", c=DC)
                cols = [d[:, :, t * P:(t + 1) * P] for d in dst]
                old = t_xT_read if kind == "x" else t_cT_read
                store_split(bank, cols, view, None, tf, list(old),
                            lambda t_hi, t_lo: t_tr.setdefault((kind, b), []).extend([t_hi, t_lo]))

            put("pool", [], lambda e: e.memset(ones[:, :], 1.0), s_const)
            put("pool", [], lambda e: e.memset(half[:, :], -0.5), s_const)
            for i in range(NST):
                put("pool", [(s_const, s_const.count)], lambda e, i=i: e.memset(raw(kst[i][ROW_MASK:P, :, :]), 1.0), s_const)
                put("pool", [(s_const, s_const.count)], lambda e, i=i: e.memset(raw(qst[i][ROW_MASK:P, :, :]), 1.0), s_const)
            t_const = (s_const, s_const.count)

            s_w_in = [sem(f"s_w_in{i}") for i in range(NP_)]
            s_w_hi, s_w_lo = sem("s_w_hi"), sem("s_w_lo")
            stage_free = [[] for _ in range(NP_)]
            t_w, staged = {}, [0]

            def split_weight(w, c, stage, t_in):
                t_hi = put("act", [t_in], lambda e: e.activation(w_hi[w][:, c, :], stage[:, :], ACT.Copy), s_w_hi)
                t_lo = put("dve", [t_in, t_hi], lambda e: e.tensor_tensor(
                    w_lo[w][:, c, :], stage[:, :], raw(w_hi[w][:, c, :]), ALU.subtract), s_w_lo)
                t_w[w] = [t_hi, t_lo]
                return [t_hi, t_lo]

            def load_weight(w, src):
                def chunk(c):
                    slot = staged[0] % NP_
                    staged[0] += 1
                    t_in = put("sp", stage_free[slot], lambda e: e.dma_start(
                        p_ring[slot][:, :], src[c * P:(c + 1) * P, :]), s_w_in[slot], 16)

                    def split():
                        stage_free[slot] = split_weight(w, c, p_ring[slot], t_in)
                    return split
                return [chunk(c) for c in range(DC)]

            def load_wo(c):
                slot = x_turn[0] % NX
                x_turn[0] += 1
                t_in = put("pool", x_in_free[slot], lambda e: e.dma_start(
                    x_in[slot][:, :], Wo[c * P:(c + 1) * P, :]), s_x_in[slot], 16)
                wo_steps.append(lambda: x_in_free.__setitem__(slot, split_weight("o", c, x_in[slot], t_in)))

            wo_steps = []

            for t in range(TB):
                load_tile("c", 0, t)
            wk_steps = load_weight("k", Wk)
            for t in range(TB):
                transpose_tile("c", 0, t)
                flush()
                wk_steps[t]()

            put("sp", [], lambda e: e.dma_start(ws_sb[:, :, 0:E], Ws.rearrange("(c p) n -> p c n", p=P)), s_bias_in, 16)
            put("sp", [], lambda e: e.dma_start(bs_b[:, :], bs.rearrange("(a n) -> a n", a=1).to_broadcast([P, E])), s_bias_in, 16)
            put("sp", [], lambda e: e.dma_start(bo_b[:, :], bo.rearrange("(a n) -> a n", a=1).to_broadcast([P, D])), s_bias_in, 16)
            for n, v in enumerate((bq, bk, bv)):
                put("sp", [], lambda e, n=n, v=v: e.dma_start(
                    bias_rows[n * DC:(n + 1) * DC, :], v.rearrange("(c p) -> c p", p=P)), s_bias_in, 16)
            put("sp", [], lambda e: e.dma_start(mask_u8, mask), s_bias_in, 16)
            t_bias_in = (s_bias_in, s_bias_in.count)
            for t in range(TB):
                load_tile("x", 0, t)
            t_ws0 = put("pool", [t_const], lambda e: e.memset(ws_sb[:, :, E:QUAD], 0.0), s_const)

            s_mask = sem("s_mask")
            t = put("dve", [t_bias_in], lambda e: e.tensor_scalar(
                mask_neg, mask_u8, 1.0, MASKED, ALU.subtract, ALU.mult), s_mask)
            s_mask_store = sem("s_mask_store")
            t_mask = put("sp", [t], lambda e: e.dma_start(raw(mask_rows), mask_neg), s_mask_store, 16)

            mask_any = sb(p1, "mask_any", [B, 1])
            mask_diag = sb(p1, "mask_diag", [B, B])
            s_any = sem("s_any")
            t_ones_b = put("dve", [], lambda e: e.memset(ones_b, SCALE), s_any)
            t_any = put("dve", [t_bias_in], lambda e: e.reduce_max(mask_any[:, :], mask_u8, AX.X), s_any)
            t_any = put("dve", [t_any, t_ident], lambda e: e.tensor_scalar(
                mask_diag[:, :], ident[0:B, 0:B], mask_any[:, 0:1], None, ALU.mult), s_any)
            bank, free = take_bank()
            t = put("pe", free + [t_any, t_ones_b], lambda e, bank=bank: e.matmul(
                ps_gen[bank][:, 0:B], lhsT=ones_b, rhs=mask_diag[:, :], start=True, stop=True), s_gen)
            t_keep = put("dve", [t], lambda e, bank=bank: e.tensor_copy(keep_scale[:, :], ps_gen[bank][:, 0:B]), s_ev_dve)
            gen_free[bank] = [t_keep]
            bank, free = take_bank()
            t = put("pe", free + [t_bias_in, t_ident], lambda e, bank=bank: e.transpose(
                ps_gen[bank][:, 0:3 * DC], bias_rows, ident[0:3 * DC, 0:3 * DC]), s_gen)
            t_bias = put("dve", [t], lambda e, bank=bank: e.tensor_copy(bias_cols[:, :], ps_gen[bank][:, 0:3 * DC]), s_ev_dve)
            gen_free[bank] = [t_bias]

            wq_steps = load_weight("q", Wq)
            for t in range(TB):
                normalise_tile(0, t)
                flush()
                transpose_tile("x", 0, t)
                wq_steps[t]()
            flush()

            v_free = []
            t_v = {}

            def project_v(b, t):
                bank, free = take_bank()
                cols = slice(t * P, (t + 1) * P)

                tf = put("pe", free + t_tr["c", b] + t_w["v"], lambda e: three(
                    ps_gen[bank][:, :], [((cT[0][:, c, cols], cT[1][:, c, cols]),
                                          (w_hi["v"][:, c, :], w_lo["v"][:, c, :])) for c in range(DC)], e), s_gen)
                t_cT_read[:] = [tf]
                tv = put("act", [tf] + v_free, lambda e: e.activation(v_sb[:, t, :], ps_gen[bank][:, :], ACT.Copy), s_ev_act)
                gen_free[bank] = [tv]
                t_v[b] = tv

            s_stack = [{w: sem(f"s_stack_{w}{i}") for w in "qk"} for i in range(NST)]
            s_mask_row = [sem(f"s_mask_row{i}") for i in range(NST)]
            mask_of, t_mask_row = [None] * NST, [None] * NST
            stack_free = [[] for _ in range(NST)]
            t_stack = {}
            qk_free = {(w, k): [] for w in "qk" for k in ("hi", "lo")}
            s_stack_lo = [{w: sem(f"s_stack_lo_{w}{i}") for w in "qk"} for i in range(NST)]

            def project_qk(w, g):
                b, c4 = divmod(g, GB)
                k = g % NST
                src = xT if w == "q" else cT
                dst = qst[k] if w == "q" else kst[k]
                cols = slice(c4 * P, (c4 + 1) * P)
                held = {}

                def begin():
                    held["bank"], free = take_bank()
                    gen_open.add(held["bank"])
                    return free

                def finish(tf):
                    bank = held["bank"]
                    gen_open.discard(bank)
                    gen_order.remove(bank)
                    gen_order.append(bank)
                    (t_xT_read if w == "q" else t_cT_read)[:] = [tf]
                    n = ("q", "k").index(w) * DC + c4
                    store_split(bank, [qk[w, "hi"][:, :], qk[w, "lo"][:, :]], ps_gen[bank][:, :],
                                bias_cols[:, n:n + 1], tf, qk_free[w, "hi"], stack, qk_free[w, "lo"])

                def stack(*parts):
                    order = ("hi", "lo", "hi") if w == "q" else ("hi", "hi", "lo")
                    sems = {"hi": s_stack[k][w], "lo": s_stack_lo[k][w]}
                    for part in ("hi", "lo"):
                        for h in range(HG):
                            for r in range(3):
                                if order[r] != part:
                                    continue
                                put("pool" if w == "k" else "sp", [parts[("hi", "lo").index(part)], t_const] + stack_free[k],
                                    lambda e, h=h, r=r, part=part: e.dma_start(
                                        raw(dst[r * DH:(r + 1) * DH, h, :]), raw(qk[w, part][h * DH:(h + 1) * DH, :])), sems[part], 16)
                    t_hi_out, t_lo_out = [(sm, sm.count) for sm in sems.values()]
                    qk_free[w, "hi"], qk_free[w, "lo"] = [t_hi_out, parts[1]], [t_lo_out]
                    if w == "k" and mask_of[k] != b:
                        mask_of[k] = b
                        src_m = raw(mask_rows[b:b + 1, :]).rearrange("p (a n) -> p a n", a=1).to_broadcast([1, HG, SK])
                        t_mask_row[k] = put("sp", [t_mask, t_const] + stack_free[k], lambda e: e.dma_start(
                            raw(kst[k][ROW_MASK:ROW_MASK + 1, :, :]), src_m), s_mask_row[k], 16)
                    if w == "k":
                        t_stack["mask", g] = t_mask_row[k]
                    t_stack[w, g] = [t_hi_out, t_lo_out]

                def part(i):
                    free = begin() if i == 0 else []
                    wh, wl = w_hi[w][:, i, cols], w_lo[w][:, i, cols]
                    mh, ml = src[0][:, i, :], src[1][:, i, :]
                    psum = ps_gen[held["bank"]][:, :]

                    def run(e):
                        e.matmul(psum, lhsT=wh, rhs=mh, start=(i == 0), stop=False)
                        e.matmul(psum, lhsT=wh, rhs=ml, start=False, stop=False)
                        return e.matmul(psum, lhsT=wl, rhs=mh, start=False, stop=(i == DC - 1))
                    tiles = t_tr["x" if w == "q" else "c", b]
                    assert len(tiles) == 2 * TB
                    waits = free + tiles + t_w[w] if i == 0 else []
                    tf = put("pe", waits, run, s_gen)
                    if i == DC - 1:
                        finish(tf)
                return [lambda i=i: part(i) for i in range(DC)]

            s_max = sem("s_max")
            s_maxrow = [sem(f"s_maxrow{i}") for i in range(NST)]
            t_maxrow = {}
            maxes_free, nmax_free = [], []
            last_max = [None]

            def row_max(g, h, t):
                bank, free = take_bank()
                ks, qs = kst[g % NST], qst[g % NST]
                tf = put("pe", free + t_stack["q", g] + t_stack["k", g] + [t_stack["mask", g]], lambda e: e.matmul(
                    ps_gen[bank][:, :], lhsT=qs[0:ROWS_MAX, h, t * P:(t + 1) * P], rhs=ks[0:ROWS_MAX, h, :],
                    start=True, stop=True), s_gen)
                col = h * TB + t
                tm = put("dve", [tf] + maxes_free, lambda e: e.reduce_max(maxes[:, col:col + 1], ps_gen[bank][:, :], AX.X), s_max)
                gen_free[bank] = [tm]
                last_max[0] = (tf, tm)

            def max_rows(g):
                tf, tm = last_max[0]
                bank, free = take_bank()
                tt = put("pe", free + [tm, t_ident], lambda e: e.transpose(
                    ps_gen[bank][0:HG * TB, 0:P], maxes[:, :], ident[:, :]), s_gen)
                maxes_free[:] = [tt]
                view = ps_gen[bank][0:HG * TB, 0:P]
                t_hi = put("act", [tt] + nmax_free, lambda e: e.activation(nmax[0][:, :], view, ACT.Copy, scale=-1.0), s_ev_act)

                def lo():
                    t_lo = put("dve", [tt, t_hi] + nmax_free, lambda e: e.scalar_tensor_tensor(
                        nmax[1][:, :], view, -1.0, raw(nmax[0][:, :]), ALU.mult, ALU.subtract), s_ev_dve)
                    gen_free[bank] = [t_hi, t_lo]
                    gen_late.discard(bank)
                    sm = s_maxrow[g % NST]
                    for r in range(2):
                        row = ROWS_MAX + r
                        dst = qst[g % NST][row:row + 1, :, :].rearrange("p h (t n) -> p (h t) n", n=P)
                        put("pool", [t_hi, t_lo, tf], lambda e, r=r, dst=dst: e.dma_start(raw(dst), raw(nmax[r][:, :])), sm, 16)
                    nmax_free[:] = [(sm, sm.count)]
                    t_maxrow[g] = (sm, sm.count)
                gen_late.add(bank)
                deferred.append(lo)

            s_st, s_exp, s_av = sem("s_st"), sem("s_exp"), sem("s_av")
            p_free = [[] for _ in range(NP_)]
            p_slot = {}
            sc_turn = [0]

            def scores(g, kt, h):
                ks, qs = kst[g % NST], qst[g % NST]
                slot = sc_turn[0] % NP_
                bank, free = take_bank()
                sc_turn[0] += 1
                ts = put("pe", free + [t_maxrow[g]], lambda e: e.matmul(
                    ps_gen[bank][:, :], lhsT=ks[0:ROWS_ALL, h, kt * P:(kt + 1) * P], rhs=qs[0:ROWS_ALL, h, :],
                    start=True, stop=True), s_st)
                if kt == KT - 1:
                    stack_free[g % NST] = [ts]
                b = g // GB
                te = put("act", [ts, t_keep] + p_free[slot], lambda e: e.activation(
                    p_ring[slot][:, :], ps_gen[bank][:, :], ACT.Exp, scale=keep_scale[:, b:b + 1]), s_exp)
                gen_free[bank] = [te]
                p_slot[g, kt, h] = (slot, te)

            att_free = []
            t_oT = {}
            oT_free = []
            s_nrm, s_oh, s_ol = sem("s_nrm"), sem("s_oh"), sem("s_ol")
            s_rd = sem("s_rd")
            soon = []
            nrm_free = [t_mask, t_bias, t_keep]

            def attend(g, kt, psum):
                b, c4 = divmod(g, GB)
                slots = [p_slot[g, kt, h] for h in range(HG)]

                def run(e):
                    for h in range(HG):
                        w = v_sb[:, kt, (c4 * HG + h) * DH:(c4 * HG + h + 1) * DH] if psum is ps_att else ones[:, :]
                        last = e.matmul(psum[h * DH:(h + 1) * DH, :], lhsT=w, rhs=p_ring[slots[h][0]][:, :],
                                        start=(kt == 0), stop=(kt == KT - 1))
                    return last
                ta = put("pe", [s[1] for s in slots] + [t_v[b], t_const] + (list(att_free) if kt == 0 else []), run, s_av)
                for s in slots:
                    p_free[s[0]] = [ta]
                if psum is ps_att:
                    return
                if kt < KT - 1:
                    return
                if c4 == GB - 1:
                    v_free[:] = [ta]
                tc = put("act", [ta] + nrm_free, lambda e: e.activation(rden[:, :], ps_den[:, :], ACT.Copy), s_nrm)
                ta = put("act", [ta] + nrm_free, lambda e: e.activation(att_n[:, :], ps_att[:, :], ACT.Copy), s_nrm)
                att_free[:] = [ta]
                tr = []

                def quarter(n):
                    c = slice(n * P, (n + 1) * P)
                    t = put("dve", [tc], lambda e: e.reciprocal(rden[:, c], rden[:, c]), s_rd)
                    tr[:] = [t]

                def divide():
                    tr[:] = [put("dve", [ta] + tr, lambda e: e.tensor_tensor(att_n[:, :], att_n[:, :], rden[:, :], ALU.mult), s_rd)]

                def split_output():
                    tn = tr[0]
                    bias = bias_cols[:, 2 * DC + c4:2 * DC + c4 + 1]
                    free = list(oT_free)
                    th = put("act", [tn, t_bias] + free, lambda e: e.activation(
                        oT[0][:, c4, :], att_n[:, :], ACT.Identity, bias=bias), s_oh)

                    def lo():
                        tl = put("dve", [tn, th] + free, lambda e: e.scalar_tensor_tensor(
                            oT[1][:, c4, :], att_n[:, :], bias, raw(oT[0][:, c4, :]), ALU.add, ALU.subtract), s_ol)
                        nrm_free[:] = [th, tl]
                        t_oT[b] = [th, tl]
                    deferred.append(lo)
                soon.extend([lambda n=n: quarter(n) for n in range(S // P)] + [divide, lambda: None, split_output])

            s_x1 = sem("s_x1")
            t_hn = {}

            residual = {}

            def load_residual(b, t):
                rows = slice((b * TB + t) * P, (b * TB + t + 1) * P)
                xs = x_turn[0] % NX
                x_turn[0] += 1
                tr = put("pool", x_in_free[xs], lambda e: e.dma_start(x_in[xs][:, :], x_tok[rows, :]), s_x_in[xs], 16)
                residual[b, t] = (xs, tr)

            def add_bias(b, t):
                xs, tr = residual[b, t]
                tr = put("pool", [tr, t_bias_in], lambda e: e.tensor_tensor(x_in[xs][:, :], x_in[xs][:, :], bo_b[:, :], ALU.add), s_x1)
                residual[b, t] = (xs, tr)

            def output_tile(b, t):
                while soon:
                    soon.pop(0)()
                flush()
                n = b * TB + t
                rows = slice(n * P, (n + 1) * P)
                xs, tr = residual[b, t]
                x1 = x_in[xs]
                bank, free = take_bank()
                cols = slice(t * P, (t + 1) * P)
                tf = put("pe", free + t_oT[b] + t_w["o"], lambda e: three(
                    ps_gen[bank][:, :], [((oT[0][:, c, cols], oT[1][:, c, cols]),
                                          (w_hi["o"][:, c, :], w_lo["o"][:, c, :])) for c in range(GB)], e), s_gen)
                oT_free[:] = [tf]
                t1 = put("dve", [tf, tr], lambda e: e.tensor_tensor(
                    x1[:, :], ps_gen[bank][:, :], x1[:, :], ALU.add), s_ev_dve)
                gen_free[bank] = [t1]
                ts = put("sp", [t1], lambda e: e.dma_start(out_tok[rows, :], x1[:, :]), s_x1_store, 16)

                def store_row(th):
                    tsh = put("sp", [th], lambda e: e.dma_start(hn_rows[rows, 0:D], x1[:, :]), s_hn_store, 16)
                    t_hn[n] = (xs, th, tsh)
                layernorm(x1[:, :], x1[:, :], [t1], lambda: [ts], store_row)

            s_hnT, s_lg = sem("s_hnT"), sem("s_lg")
            hnT_free, held_lg = [], {}

            held_hnT = {}

            def route_tile(b, t):
                n = b * TB + t
                slot, th, tsh = t_hn[n]
                bank, free = take_bank()

                def run(e):
                    for c in range(DC):
                        last = e.transpose(ps_gen[bank][:, c * P:(c + 1) * P], x_in[slot][:, c * P:(c + 1) * P], ident[:, :])
                    return last
                tf = put("pe", free + [th], run, s_gen)
                x_in_free[slot] = [tf, tsh]
                tc = put("act", [tf] + hnT_free, lambda e: e.activation(
                    hnT[:, :, :], ps_gen[bank][:, :].rearrange("p (c t) -> p c t", c=DC), ACT.Copy), s_ev_act)
                gen_free[bank] = [tc]
                held_hnT[n] = tc

            def logits_tile(b, t):
                n = b * TB + t
                bank, free = take_bank()

                def run(e):
                    for c in range(DC):
                        last = e.matmul(ps_gen[bank][c * QUAD:(c + 1) * QUAD, 0:P], lhsT=ws_sb[:, c, :], rhs=hnT[:, c, :],
                                        start=True, stop=True)
                    return last
                tf = put("pe", free + [held_hnT[n], t_bias_in, t_ws0], run, s_gen)
                lgT = hnT[:, 0, :]
                held_lg[n] = put("act", [tf], lambda e: e.activation(
                    lgT, ps_gen[bank][:, 0:P], ACT.Copy), s_ev_act)
                gen_free[bank] = [held_lg[n]]

            def logits_back(b, t):
                n = b * TB + t
                bank, free = take_bank()
                tf = put("pe", free + [held_lg[n]], lambda e: e.transpose(ps_gen[bank][:, 0:P], hnT[:, 0, :], ident[:, :]), s_gen)
                hnT_free[:] = [tf]
                parts = ps_gen[bank][:, 0:P].rearrange("p (c w) -> p w c", w=QUAD)[:, 0:E, :]
                ts = put("dve", [tf], lambda e: e.reduce_sum(probs[:, n, :], parts, AX.X), s_ev_dve)
                gen_free[bank] = [ts]
                tl = put("dve", [ts], lambda e: e.tensor_tensor(probs[:, n, :], probs[:, n, :], bs_b[:, :], ALU.add), s_lg)
                if t == TB - 1:
                    softmax_rows(b, tl)

            def softmax_rows(b, t):
                v = probs[:, b * TB:(b + 1) * TB, :]
                def wide(a):
                    return a[:, :].rearrange("p (t a) -> p t a", a=1).to_broadcast([P, TB, E])
                t = put("dve", [t], lambda e: e.reduce_max(rt_max[:, :], v, AX.X), s_lg)
                t = put("dve", [t], lambda e: e.tensor_tensor(v, v, wide(rt_max), ALU.subtract), s_lg)
                t = put("act", [t], lambda e: e.activation(v, v, ACT.Exp), s_hnT)
                t = put("dve", [t], lambda e: e.reduce_sum(rt_sum[:, :], v, AX.X), s_lg)
                t = put("dve", [t], lambda e: e.reciprocal(rt_sum[:, :], rt_sum[:, :]), s_lg)
                t = put("dve", [t], lambda e: e.tensor_tensor(v, v, wide(rt_sum), ALU.mult), s_lg)
                rows = hn_rows[b * S:(b + 1) * S, D:D + E].rearrange("(t p) e -> p t e", p=P)
                put("sp", [t], lambda e: e.dma_start(rows, v), s_probs_store, 16)
                return t

            GAPS = 5 * KT
            places = []

            def place(a, b, steps):
                for k, step in enumerate(steps):
                    places.append((a + (b - a) * (k + 0.5) / len(steps), step))

            def each(f, *args):
                return [lambda t=t: f(*args, t) for t in range(TB)]

            for i in range(2, NG):
                k_at, q_at = {2: ((0.0, 0.13), (0.3, 0.45)), 0: ((0.0, 0.14), (0.26, 0.42))}.get(i % GB, ((0.03, 0.22), (0.23, 0.42)))
                place(i - 2 + k_at[0], i - 2 + k_at[1], project_qk("k", i))
                place(i - 2 + q_at[0], i - 2 + q_at[1], project_qk("q", i))
            for i in range(1, NG):
                place(i - 1 + (0.0 if i % GB == 0 else -0.1), i - 1 + 0.68, [lambda h=h, t=t, i=i: row_max(i, h, t) for h in range(HG) for t in range(TB)])
                place(i - 1 + 0.71, i - 1 + 0.74, [lambda i=i: max_rows(i)])
            for b in range(B):
                i = b * GB
                place(i + 0.13, i + 0.28, each(project_v, b))
                if b > 0:
                    place(i - 3 - 0.1, i - 3 + 0.22, each(load_tile, "c", b))
                    place(i - 3 + 0.5, i - 3 + 0.9, each(transpose_tile, "c", b))
                    place(i - 3 + 0.6, i - 3 + 0.95, each(load_tile, "x", b))
                    place(i - 3 + 0.8, i - 2 + 0.15, each(normalise_tile, b))
                    place(i - 2, i - 2 + 0.24, each(transpose_tile, "x", b))
            for b in range(B - 1):
                at = (b + 1) * GB + 0.5
                for step, shift in ((load_residual, -0.24), (add_bias, -0.12), (output_tile, 0.0), (route_tile, 0.15),
                                    (logits_tile, 0.21), (logits_back, 0.27)):
                    place(at + shift, at + shift + 0.52, each(step, b))
            place(0.0, 0.3, [lambda c=c: load_wo(c) for c in range(DC)])
            place(0.4, 0.85, [lambda c=c: wo_steps[c]() for c in range(DC)])
            places.sort(key=lambda p: p[0])

            for step in project_qk("k", 0) + project_qk("q", 0) + project_qk("k", 1) + project_qk("q", 1) :
                step()
                flush()
            wv_steps = load_weight("v", Wv)
            for h in range(HG):
                for t in range(TB):
                    row_max(0, h, t)
                wv_steps[h]()
            max_rows(0)
            flush()

            def fill(time):
                flush()
                if soon:
                    soon.pop(0)()
                while places and places[0][0] < time:
                    places.pop(0)[1]()

            for i in range(NG):
                for kt in range(KT):
                    before = (i, kt - 1) if kt else (i - 1, KT - 1)
                    time = [i + (5 * kt + n) / GAPS for n in range(1, 6)]
                    scores(i, kt, 0)
                    scores(i, kt, 1)
                    fill(time[0])
                    if before[0] >= 0:
                        attend(*before, ps_att)
                    fill(time[1])
                    if before[0] >= 0:
                        attend(*before, ps_den)
                    scores(i, kt, 2)
                    fill(time[2])
                    scores(i, kt, 3)
                    fill(time[3])
                    fill(time[4])
                flush()
            attend(NG - 1, KT - 1, ps_att)
            attend(NG - 1, KT - 1, ps_den)
            while soon:
                soon.pop(0)()
            flush()
            for t in range(2):
                load_residual(B - 1, t)
                add_bias(B - 1, t)
            for t in range(TB):
                if t + 2 < TB:
                    load_residual(B - 1, t + 2)
                    add_bias(B - 1, t + 2)
                output_tile(B - 1, t)
                flush()
                for f in (route_tile, logits_tile, logits_back):
                    f(B - 1, t)
            t_probs = (s_lg, s_lg.count)
            t_x1_all = [(s_x1_store, s_x1_store.count)]
            t_hn_all = [(s, s.count) for s in (s_hn_store, s_probs_store)]
            t_part1 = [(s, s.count) for s in (s_gen, s_st, s_av, s_ev_act, s_ev_dve, s_exp, s_oh, s_ol, s_nrm, s_rd,
                                              s_norm, s_hnT, s_lg, s_x1)] + t_x1_all + t_hn_all

        gate_stack = top
        idx = sb(gate_stack, "idx", [P, E, K // P], I32)
        HALF = E // 2
        A_N, B_N = QUAD, K // QUAD
        with ExitStack() as p2:
            s_go = sem("s_go")
            pT = sb(p2, "pT", [P, 2 * P])
            expert_of = sb(p2, "expert_of", [P, E])
            same = sb(p2, "same", [P, P], BF16)
            tri = sb(p2, "tri", [P, P], BF16)
            ones_h = sb(p2, "ones_h", [P, P], BF16)
            ones_f = sb(p2, "ones_f", [P, P])
            junk = sb(p2, "junk", [P, 2 * P], BF16)
            cnt = sb(p2, "cnt", [P, 1], F32)
            cnt_h = sb(p2, "cnt_h", [P, 1], BF16)
            thr = sb(p2, "thr", [P, 1], I32)
            cand = sb(p2, "cand", [P, 1], I32)
            okc = sb(p2, "okc", [P, 1])
            thr_d = sb(p2, "thr_d", [P, E])
            thr_b = sb(p2, "thr_b", [P, E])
            marks = sb(p2, "marks", [P, 2, NT, E], BF16)
            tot = [sb(p2, f"tot{i}", [P, 2, NT, E]) for i in range(2)]
            first = sb(p2, "first", [P, 2, NT, E])
            slot_f = sb(p2, "slot_f", [P, NT, E])
            slot_e = sb(p2, "slot_e", [P, NT, E])
            slot_i = sb(p2, "slot_i", [P, NT, E], I32)
            sa = sb(p2, "sa", [P, NT, E], I32)
            sbb = sb(p2, "sbb", [P, NT, E], I32)
            sa_h = sb(p2, "sa_h", [P, NT, E], F16)
            sb_h = sb(p2, "sb_h", [P, NT, E], F16)
            iota = sb(p2, "iota", [P, QUAD], F16)
            tok = sb(p2, "tok", [P, NT], F16)
            hot_a = sb(p2, "hot_a", [P, NT * E, A_N], F16)
            hot_b = sb(p2, "hot_b", [P, NT * E, B_N], F16)
            s_c2, s_sel, s_cnt, s_tot2 = sem("s_c2"), sem("s_sel"), sem("s_cnt"), sem("s_tot2")

            def dve(waits, run):
                return put("dve", waits, run, s_sel)

            TOK0 = N // 2
            put("pool", t_part1, lambda e: e.iota(iota[:, :], pattern=[[1, QUAD]], base=0, channel_multiplier=0,
                                                  allow_small_or_imprecise_dtypes=True), s_c2)
            put("pool", [(s_c2, s_c2.count)], lambda e: e.iota(tok[:, :], pattern=[[P, NT]], base=-TOK0, channel_multiplier=1,
                                             allow_small_or_imprecise_dtypes=True), s_c2)
            put("pool", [(s_c2, s_c2.count)], lambda e: e.memset(ones_h[:, :], 1.0), s_c2)
            put("pool", [(s_c2, s_c2.count)], lambda e: e.memset(ones_f[:, :], 1.0), s_c2)
            t = (s_c2, s_c2.count)
            put("pool", [t], lambda e: e.affine_select(out=tri[:, :], in_=ones_h[:, :], compare_op=ALU.is_ge, fill=0.0,
                                                       base=0, pattern=[[1, P]], channel_multiplier=-1), s_c2)
            t_c2 = (s_c2, s_c2.count)
            t = dve(t_part1, lambda e: e.reduce_max(expert_of[:, :], ident[:, :].rearrange("p (t e) -> p e t", e=E), AX.X))
            t_same = dve([t], lambda e: e.tensor_copy(
                same[:, :].rearrange("p (t e) -> p t e", e=E),
                expert_of[:, :].rearrange("p (a e) -> p a e", a=1).to_broadcast([P, P // E, E])))
            t_thr0 = dve([], lambda e: e.memset(thr[:, :], 0))

            bank, free = take_bank()

            def run(e):
                for r in range(2):
                    last = e.transpose(ps_gen[bank][:, r * P:(r + 1) * P],
                                       probs[:, r * 16:(r + 1) * 16, :].rearrange("p t e -> p (t e)"), ident[:, :])
                return last
            t = put("pe", free + t_part1, run, s_gen)
            t_pT = dve([t], lambda e: e.tensor_copy(pT[:, :], ps_gen[bank][:, 0:2 * P]))

            t_thr = t_thr0
            for bit in range(29, -1, -1):
                t = dve([t_thr], lambda e, bit=bit: e.tensor_single_scalar(cand[:, :], thr[:, :], 1 << bit, ALU.bitwise_or))
                t = dve([t, t_pT], lambda e: e.tensor_scalar(
                    junk[:, :], pT[:, :], cand[:, 0:1].bitcast(F32), 0.0, ALU.is_ge, ALU.add, accum_out=cnt[:, :]))
                t = dve([t], lambda e: e.tensor_copy(cnt_h[:, :], cnt[:, :]))
                t = put("pe", [t, t_same], lambda e: e.matmul(ps_den[:, 0:1], lhsT=same[:, :], rhs=cnt_h[:, :], start=True, stop=True), s_cnt)
                t = dve([t], lambda e: e.scalar_tensor_tensor(
                    okc[:, :], ps_den[:, 0:1], float(K), cand[:, :].bitcast(F32), ALU.is_ge, ALU.mult))
                t_thr = dve([t], lambda e: e.tensor_tensor(thr[:, :].bitcast(F32), thr[:, :].bitcast(F32), okc[:, :], ALU.max))

            t = dve([t_thr], lambda e: e.tensor_scalar(thr_d[:, :], ident[:, 0:E], thr[:, 0:1].bitcast(F32), None, ALU.mult))
            t = put("pe", [t, t_c2], lambda e: e.matmul(ps_den[:, 0:E], lhsT=ones_f[:, :], rhs=thr_d[:, :], start=True, stop=True), s_cnt)
            t = dve([t], lambda e: e.tensor_copy(thr_b[:, :], ps_den[:, 0:E]))
            wide_thr = thr_b[:, :].rearrange("p (a e) -> p a e", a=1).to_broadcast([P, NT, E])
            dve([t], lambda e: e.tensor_tensor(marks[:, 0, :, :], probs[:, :, :], wide_thr, ALU.is_gt))
            t_marks = dve([], lambda e: e.tensor_tensor(marks[:, 1, :, :], probs[:, :, :], wide_thr, ALU.is_equal))
            flat = marks[:, :, :, :].rearrange("p m t e -> p (m t e)")
            t_in = put("pe", [t_marks, t_c2], lambda e: e.matmul(ps_att[:, :], lhsT=tri[:, :], rhs=flat, start=True, stop=True), s_tot2)
            t_tt = put("pe", [], lambda e: e.matmul(ps_den[:, :], lhsT=ones_h[:, :], rhs=flat, start=True, stop=True), s_tot2)
            merged = "p m t e -> p (m t e)"
            t = dve([t_tt], lambda e: e.tensor_copy(tot[0][:, :, :, :].rearrange(merged), ps_den[:, :]))
            t_first = dve([t], lambda e: e.tensor_copy(first[:, :, :, :], tot[0][:, :, :, :]))
            t = t_first
            step, cur = 1, 0
            while step < NT:
                a, b_ = tot[cur], tot[1 - cur]
                dve([t], lambda e, a=a, b_=b_, s=step: e.tensor_copy(b_[:, :, 0:s, :], a[:, :, 0:s, :]))
                t = dve([], lambda e, a=a, b_=b_, s=step: e.tensor_tensor(
                    b_[:, :, s:NT, :], a[:, :, s:NT, :], a[:, :, 0:NT - s, :], ALU.add))
                step, cur = 2 * step, 1 - cur
            run_tot, rank = tot[cur], tot[1 - cur]
            t = dve([t], lambda e: e.tensor_tensor(first[:, :, :, :], run_tot[:, :, :, :], first[:, :, :, :], ALU.subtract))
            t = dve([t, t_in], lambda e: e.tensor_tensor(rank[:, :, :, :].rearrange(merged), ps_att[:, :], first[:, :, :, :].rearrange(merged), ALU.add))
            above = run_tot[:, 0, NT - 1:NT, :].to_broadcast([P, NT, E])
            t = dve([t], lambda e: e.tensor_tensor(slot_e[:, :, :], rank[:, 1, :, :], above, ALU.add))
            t = dve([t], lambda e: e.tensor_tensor(slot_e[:, :, :], slot_e[:, :, :], marks[:, 1, :, :], ALU.mult))
            t = dve([t], lambda e: e.tensor_tensor(slot_f[:, :, :], rank[:, 0, :, :], marks[:, 0, :, :], ALU.mult))
            t = dve([t], lambda e: e.tensor_tensor(slot_f[:, :, :], slot_f[:, :, :], slot_e[:, :, :], ALU.add))
            t = dve([t], lambda e: e.tensor_scalar(slot_i[:, :, :], slot_f[:, :, :], -1.0, None, ALU.add))
            dve([t], lambda e: e.tensor_single_scalar(sa[:, :, :], slot_i[:, :, :], A_N - 1, ALU.bitwise_and))
            t = dve([], lambda e: e.tensor_single_scalar(sbb[:, :, :], slot_i[:, :, :], 5, ALU.arith_shift_right))
            dve([t], lambda e: e.tensor_copy(sa_h[:, :, :], sa[:, :, :]))
            t = dve([], lambda e: e.tensor_copy(sb_h[:, :, :], sbb[:, :, :]))

            def spread(a, n):
                return a[:, :, :].rearrange("p t e -> p (t e)").rearrange("p (c a) -> p c a", a=1).to_broadcast([P, NT * E, n])

            def count(n):
                return iota[:, 0:n].rearrange("p (a n) -> p a n", a=1).to_broadcast([P, NT * E, n])
            t_b = dve([t, t_c2], lambda e: e.tensor_tensor(hot_b[:, :, :], spread(sb_h, B_N), count(B_N), ALU.is_equal))
            view = hot_b[:, :, :].rearrange("p (t e) b -> p t (e b)", e=E)
            t_b = dve([t_b], lambda e: e.tensor_tensor(
                view, view, tok[:, :].rearrange("p (t a) -> p t a", a=1).to_broadcast([P, NT, E * B_N]), ALU.mult))
            t_a = dve([], lambda e: e.tensor_tensor(hot_a[:, :, :], spread(sa_h, A_N), count(A_N), ALU.is_equal))
            t_idx = None
            for hf in range(2):
                psum = ps_gen[hf]

                def run(e, hf=hf, psum=psum):
                    for n in range(NT):
                        c = slice(n * E + hf * HALF, n * E + (hf + 1) * HALF)
                        last = e.matmul(psum[:, 0:HALF * B_N], lhsT=hot_a[:, c, :].rearrange("p e a -> p (e a)"),
                                        rhs=hot_b[:, c, :].rearrange("p e b -> p (e b)"), start=(n == 0), stop=(n == NT - 1))
                    return last
                t = put("pe", [t_a, t_b, t_pT], run, s_cnt)
                for e4 in range(HALF):
                    for r in range(P // QUAD):
                        srcv = psum[e4 * QUAD:(e4 + 1) * QUAD, e4 * B_N + r:(e4 + 1) * B_N:P // QUAD]
                        t_idx = dve([t], lambda e, srcv=srcv, r=r, k=hf * HALF + e4: e.tensor_scalar(
                            idx[r * QUAD:(r + 1) * QUAD, k, :], srcv, float(TOK0), None, ALU.add))

        FB = 2 * P
        NPIECE = F // FB
        NF = F // P
        TT = K // P
        with ExitStack() as p3:
            NR, NS = 3, 3
            w1_raw = [sb(p3, f"w1_raw{i}", [P, DC, FB]) for i in range(NR)]
            w2_raw = [sb(p3, f"w2_raw{i}", [P, 2, D]) for i in range(NR)]
            w1s = [[sb(p3, f"w1_{k}{i}", [P, DC, FB], F32R) for k in ("hi", "lo")] for i in range(NS)]
            w2s = [[sb(p3, f"w2_{k}{i}", [P, 2, D], F32R) for k in ("hi", "lo")] for i in range(NS)]
            rows = [sb(p3, f"rows{i}", [P, ROW]) for i in range(2 * TT)]
            hT = [[sb(p3, f"hT_{k}{i}", [P, DC, K], F32R) for k in ("hi", "lo")] for i in range(2)]
            gel = [sb(p3, f"gel{i}", [P, K]) for i in range(2)]
            gel_s = [[sb(p3, f"gel_{k}{i}", [P, K], F32R) for k in ("hi", "lo")] for i in range(2)]
            b2_b = [sb(p3, f"b2_b{i}", [P, D]) for i in range(2)]
            y_sb = [sb(p3, f"y_sb{i}", [P, D]) for i in range(TT)]
            y_out = [sb(p3, f"y_out{i}", [P, D]) for i in range(TT)]
            b1_raw = sb(p3, "b1_raw", [P, P])
            b1_cols = sb(p3, "b1_cols", [P, P])

            t_part2 = [t_idx, (s_cnt, s_cnt.count), (s_tot2, s_tot2.count), t_c2]
            s_w1_in = [sem(f"s_w1_in{i}") for i in range(NR)]
            s_w2_in = [sem(f"s_w2_in{i}") for i in range(NR)]
            s_b1, s_b2 = sem("s_b1"), [sem(f"s_b2{i}") for i in range(2)]
            s_split = sem("s_split")
            s_rows = [sem(f"s_rows{i}") for i in range(2 * TT)]
            s_up, s_gelu, s_gel_lo, s_down = sem("s_up"), sem("s_gelu"), sem("s_gel_lo"), sem("s_down")
            s_yb, s_y, s_add = sem("s_yb"), sem("s_y"), [sem(f"s_add{i}") for i in range(TT)]
            ps_up = ps_gen
            ps_y = [p[:, :] for p in ps_gen[2:2 + TT]]
            ps_tr = [ps_att, ps_den]
            up_free, tr_free = [[], []], [[], []]
            y_free = [[] for _ in range(TT)]

            t_b1in = put("sp", t_part2 + t_part1, lambda e: e.dma_start(b1_raw[:, :], b1.rearrange("e (j p) -> (e j) p", p=P)), s_b1, 16)
            t = put("pe", [t_b1in] + t_part2, lambda e: e.transpose(ps_att[:, 0:P], b1_raw[:, :], ident[:, :]), s_gen)
            t_b1 = put("dve", [t], lambda e: e.tensor_copy(b1_cols[:, :], ps_att[:, 0:P]), s_ev_dve)
            tr_free[0] = [t_b1]

            raw_free = [[] for _ in range(NR)]
            split_free = [[[], []] for _ in range(NS)]
            pieces = [(e, j) for e in range(E) for j in range(NPIECE)]
            t_in, t_sp = {}, {}

            def load_piece(n):
                ex, j = pieces[n]
                r = n % NR
                w1v = W1[ex, :, j * FB:(j + 1) * FB].rearrange("(c p) f -> p c f", p=P)
                w2v = W2[ex, j * FB:(j + 1) * FB, :].rearrange("(c p) d -> p c d", p=P)
                ta = put("sp", raw_free[r], lambda e: e.dma_start(w1_raw[r][:, :, :], w1v), s_w1_in[r], 16)
                tb = put("sp", raw_free[r], lambda e: e.dma_start(w2_raw[r][:, :, :], w2v), s_w2_in[r], 16)
                t_in[n] = (ta, tb)

            def split_piece(n):
                r, s = n % NR, n % NS
                got = []
                for k, (rw, sp_) in enumerate(((w1_raw[r], w1s[s]), (w2_raw[r], w2s[s]))):
                    th = put("dve", [t_in[n][k]] + split_free[s][k] + t_part2, lambda e, rw=rw, sp_=sp_: e.tensor_copy(
                        sp_[0][:, :, :], rw[:, :, :]), s_split)
                    tl = put("dve", [th], lambda e, rw=rw, sp_=sp_: e.tensor_tensor(
                        sp_[1][:, :, :], rw[:, :, :], raw(sp_[0][:, :, :]), ALU.subtract), s_split)
                    got.append(tl)
                raw_free[r] = [tl]
                t_sp[n] = got

            rows_free = [[] for _ in range(2 * TT)]
            t_rows = {}

            def gather(ex):
                for tt in range(TT):
                    slot = (ex % 2) * TT + tt
                    t_rows[ex, tt] = put("pool", rows_free[slot] + [t_idx] + t_hn_all + t_part2, lambda e, slot=slot, tt=tt: e.indirect_dma_start(
                        rows[slot][:, :], None, hn_rows[:, :], bass.IndirectOffsetOnAxis(ap=idx[:, ex, tt:tt + 1], axis=0)), s_rows[slot], 16)

            hT_free = [[], []]
            t_hT = {}

            def transpose_rows(ex, tt):
                slot = (ex % 2) * TT + tt
                k = tt % 2
                psum = ps_tr[k]

                def run(e):
                    for c in range(DC):
                        last = e.transpose(psum[:, c * P:(c + 1) * P], rows[slot][:, c * P:(c + 1) * P], ident[:, :])
                    return last
                tf = put("pe", tr_free[k] + [t_rows[ex, tt]] + t_part2, run, s_gen)
                view = psum[:, :].rearrange("p (c t) -> p c t", c=DC)
                dst = [d[:, :, tt * P:(tt + 1) * P] for d in hT[ex % 2]]
                th = put("act", [tf] + hT_free[ex % 2], lambda e: e.activation(dst[0], view, ACT.Copy), s_ev_act)
                tl = put("dve", [tf, th] + hT_free[ex % 2], lambda e: e.tensor_tensor(dst[1], view, raw(dst[0]), ALU.subtract), s_ev_dve)
                tr_free[k] = [th, tl]
                t_hT[ex] = [th, tl]

            s_gfree = [[], []]
            t_gel = {}

            def up(ex, j):
                n = ex * NPIECE + j // 2
                w = w1s[n % NS]
                col = slice((j % 2) * P, (j % 2 + 1) * P)
                k = j % 2
                hh = hT[ex % 2]
                tf = put("pe", up_free[k] + [t_sp[n][0]] + t_hT[ex], lambda e: three(
                    ps_up[k][:, :], [((w[0][:, c, col], w[1][:, c, col]), (hh[0][:, c, :], hh[1][:, c, :])) for c in range(DC)], e), s_up)
                if j % 2:
                    split_free[n % NS][0] = [tf]
                if j == NF - 1:
                    hT_free[ex % 2] = [tf]
                bias = b1_cols[:, ex * NF + j:ex * NF + j + 1]
                tg = put("act", [tf, t_b1] + s_gfree[k], lambda e: e.activation(
                    gel[k][:, :], ps_up[k][:, :], ACT.Gelu_apprx_tanh, bias=bias), s_gelu)
                th = put("act", [tf, t_b1] + s_gfree[k], lambda e: e.activation(
                    gel_s[k][0][:, :], ps_up[k][:, :], ACT.Gelu_apprx_tanh, bias=bias), s_gelu)
                up_free[k] = [th]
                tl = put("dve", [th], lambda e: e.tensor_tensor(
                    gel_s[k][1][:, :], gel[k][:, :], raw(gel_s[k][0][:, :]), ALU.subtract), s_gel_lo)
                t_gel[ex, j] = [th, tl]

            def down(ex, j):
                n = ex * NPIECE + j // 2
                w = w2s[n % NS]
                k = j % 2

                def run(e):
                    for tt in range(TT):
                        c = slice(tt * P, (tt + 1) * P)
                        gh, gl = gel_s[k][0][:, c], gel_s[k][1][:, c]
                        wh, wl = w[0][:, j % 2, :], w[1][:, j % 2, :]
                        e.matmul(ps_y[tt], lhsT=gh, rhs=wh, start=(j == 0), stop=False)
                        e.matmul(ps_y[tt], lhsT=gh, rhs=wl, start=False, stop=False)
                        last = e.matmul(ps_y[tt], lhsT=gl, rhs=wh, start=False, stop=(j == NF - 1))
                    return last
                waits = [w for f in y_free for w in f] if j == 0 else []
                tf = put("pe", waits + t_gel[ex, j] + [t_sp[n][1]], run, s_down)
                s_gfree[k] = [tf]
                if j % 2:
                    split_free[n % NS][1] = [tf]
                return tf

            b2_free = [[], []]
            y_sb_free = [[] for _ in range(TT)]
            y_out_free = [[] for _ in range(TT)]
            t_b2 = {}

            def load_b2(ex):
                k = ex % 2
                t_b2[ex] = put("sp", b2_free[k] + t_part2 + t_part1, lambda e: e.dma_start(
                    b2_b[k][:, :], b2[ex:ex + 1, :].to_broadcast([P, D])), s_b2[k], 16)

            t_added = [list(t_x1_all)]

            def finish(ex, tf):
                k = ex % 2
                before = t_added[0]
                mine = []
                for tt in range(TT):
                    slot = k * TT + tt
                    ty = put("dve", [tf, t_b2[ex]] + y_sb_free[tt], lambda e, tt=tt: e.tensor_tensor(
                        y_sb[tt][:, :], ps_y[tt], b2_b[k][:, :], ALU.add), s_yb)
                    y_free[tt] = [ty]
                    to = put("act", [ty] + y_out_free[tt], lambda e, tt=tt, slot=slot: e.activation(
                        y_out[tt][:, :], y_sb[tt][:, :], ACT.Copy, scale=rows[slot][:, D + ex:D + ex + 1]), s_y)
                    y_sb_free[tt] = [to]
                    rows_free[slot] = [to]
                    ta = put("pool", [to] + before, lambda e, tt=tt: e.indirect_dma_start(
                        out_tok, bass.IndirectOffsetOnAxis(ap=idx[:, ex, tt:tt + 1], axis=0),
                        y_out[tt][:, :], None, compute_op=ALU.add), s_add[tt], 16)
                    y_out_free[tt] = [ta]
                    mine.append(ta)
                b2_free[k] = [ty]
                t_added[0] = mine

            for n in range(NR):
                if n == 0:
                    q.steps["sp"].append(([*t_part1, *t_part2], lambda e: None, None, 0))
                load_piece(n)
            gather(0)
            load_b2(0)
            split_piece(0)
            for tt in range(TT):
                transpose_rows(0, tt)
            split_piece(1)
            gather(1)
            load_b2(1)
            order = [(ex, j) for ex in range(E) for j in range(NF)]
            up(0, 0)
            for i, (ex, j) in enumerate(order):
                if i + 1 < len(order):
                    up(*order[i + 1])
                tf = down(ex, j)
                if j % 2 == 1:
                    n = i // 2
                    if n + NR < len(pieces):
                        load_piece(n + NR)
                    if n + 2 < len(pieces):
                        split_piece(n + 2)
                if ex + 1 < E and NF - 6 <= j < NF - 2:
                    transpose_rows(ex + 1, j - (NF - 6))
                if j == NF - 1:
                    finish(ex, tf)
                    if ex + 2 < E:
                        gather(ex + 2)
                        load_b2(ex + 2)
            q.steps["pool"].append((t_added[0], lambda e: None, None, 0))

        with nc.Block() as block:
            @block.sync
            def _(e):
                q.emit("sp", e)

            @block.gpsimd
            def _(e):
                q.emit("pool", e)

            @block.scalar
            def _(e):
                q.emit("act", e)

            @block.vector
            def _(e):
                q.emit("dve", e)

            @block.tensor
            def _(e):
                q.emit("pe", e)


_INS = ['x', 'ctx_1024', 'mask_BxS2_bf1', 'L0_xattn_Wq', 'L0_xattn_bq', 'L0_xattn_Wk', 'L0_xattn_bk', 'L0_xattn_Wv',
        'L0_xattn_bv', 'L0_xattn_Wo', 'L0_xattn_bo', 'L0_ffn_Ws', 'L0_ffn_bs', 'L0_ffn_W1', 'L0_ffn_b1', 'L0_ffn_W2',
        'L0_ffn_b2']


def kernel(**inputs):
    import numpy as np
    import concourse.bacc as bacc
    from concourse.bass_utils import run_bass_kernel_spmd

    nc = bacc.Bacc("TRN2", target_bir_lowering=False, num_devices=1)
    arrays, args = {}, []
    for name in _INS:
        a = np.ascontiguousarray(inputs[name])
        arrays[f"in_{name}"] = a
        args.append(nc.dram_tensor(f"in_{name}", a.shape, mybir.dt.from_np(a.dtype), kind="ExternalInput").ap())
    b, s, d = inputs['x'].shape
    e = inputs['L0_ffn_Ws'].shape[1]
    out = nc.dram_tensor("out_x", (b, s, d), F32, kind="ExternalOutput").ap()
    hn_rows = nc.dram_tensor("hn_rows", (b * s, d + e), F32, kind="Internal").ap()
    mask_rows = nc.dram_tensor("mask_rows", inputs['mask_BxS2_bf1'].shape, F32R, kind="Internal").ap()
    attention_moe_kernel(nc, *args, out, hn_rows, mask_rows)
    r = run_bass_kernel_spmd(nc, [arrays], core_ids=[0])
    return r.results[0]["out_x"]
```

```python
from contextlib import ExitStack

import concourse.bass as bass
from concourse import mybir

F32 = mybir.dt.float32
F32R = mybir.dt.float32r
BF16 = mybir.dt.bfloat16
F16 = mybir.dt.float16
I32 = mybir.dt.int32
U8 = mybir.dt.uint8
ALU = mybir.AluOpType
ACT = mybir.ActivationFunctionType
AX = mybir.AxisListType

P = 128
QUAD = 32
BANK = 512
MASKED = 2.0 ** 100


class Sem:

    def __init__(self, ctx, nc, name):
        self.sem = ctx.enter_context(nc.semaphore(name))
        self.count = 0


class Queues:

    def __init__(self):
        self.steps = {"pe": [], "act": [], "dve": [], "pool": [], "sp": []}

    def put(self, engine, waits, run, done=None, by=1):
        if done is not None:
            done.count += by
        self.steps[engine].append((list(waits), run, done, by))
        return None if done is None else (done, done.count)

    def emit(self, engine, handle):
        reached = {}
        for waits, run, done, by in self.steps[engine]:
            for sem, value in waits:
                if reached.get(id(sem), 0) < value:
                    handle.wait_ge(sem.sem, value)
                    reached[id(sem)] = value
            last = run(handle)
            if done is not None:
                last.then_inc(done.sem, by)


def attention_moe_kernel(nc, x, ctx_in, mask, Wq, bq, Wk, bk, Wv, bv, Wo, bo,
                         Ws, bs, W1, b1, W2, b2, out, hn_rows, mask_rows):
    B, S, D = x.shape
    SK = ctx_in.shape[1]
    E = Ws.shape[1]
    F = W1.shape[2]
    DH = QUAD
    H = D // DH
    N = B * S
    K = N // E
    DC = D // P
    TB = S // P
    KT = SK // P
    NT = N // P
    HG = P // DH
    GB = H // HG
    NG = B * GB
    SCALE = float(DH) ** -0.5
    EPS = 1e-5
    ROW = hn_rows.shape[1]
    assert S == SK == D == K == BANK and E == 8 and H == 16 and P == 8 * 16

    x_tok = x.rearrange("b s d -> (b s) d")
    ctx_tok = ctx_in.rearrange("b s d -> (b s) d")
    out_tok = out.rearrange("b s d -> (b s) d")
    q = Queues()
    put = q.put

    with ExitStack() as top:
        def sem(name):
            return Sem(top, nc, name)

        def sb(scope, name, shape, dt=F32):
            return scope.enter_context(nc.sbuf_tensor(name, shape, dt))

        NGEN = 6
        ps_att = top.enter_context(nc.psum_tensor("ps_att", [P, BANK], F32))
        ps_den = top.enter_context(nc.psum_tensor("ps_den", [P, BANK], F32))
        ps_gen = [top.enter_context(nc.psum_tensor(f"ps_gen{i}", [P, BANK], F32)) for i in range(NGEN)]

        ident = sb(top, "ident", [P, P])
        probs = sb(top, "probs", [P, NT, E])
        s_const = sem("s_const")
        s_bias_in = sem("s_bias_in")

        put("pool", [], lambda e: e.memset(ident[:, :], 0.0), s_const)
        t_zero = (s_const, s_const.count)
        t_ident = put("pool", [t_zero], lambda e: e.affine_select(
            out=ident[:, :], in_=ident[:, :], compare_op=ALU.not_equal, fill=1.0, base=0,
            pattern=[[-1, P]], channel_multiplier=1), s_const)

        gen_free = [[] for _ in range(NGEN)]
        gen_order = list(range(NGEN))
        deferred = []

        def flush():
            while deferred:
                deferred.pop(0)()
        gen_open = set()
        gen_late = set()

        def take_bank():
            i = next(k for k in gen_order if k not in gen_open)
            gen_order.remove(i)
            gen_order.append(i)
            if i in gen_late:
                flush()
            waits, gen_free[i] = gen_free[i], []
            return i, waits

        s_gen = sem("s_gen")
        s_ev_act = sem("s_ev_act")
        s_ev_dve = sem("s_ev_dve")

        def raw(ap):
            return ap.bitcast(F32)

        def three(psum, pairs, e):
            n = len(pairs)
            for i, ((wh, wl), (mh, ml)) in enumerate(pairs):
                e.matmul(psum, lhsT=wh, rhs=mh, start=(i == 0), stop=False)
                e.matmul(psum, lhsT=wh, rhs=ml, start=False, stop=False)
                last = e.matmul(psum, lhsT=wl, rhs=mh, start=False, stop=(i == n - 1))
            return last

        NX = 4
        s_hn_store = [sem(f"s_hn_store{i}") for i in range(NX)]
        s_probs_store = sem("s_probs_store")
        s_x1_store = [sem(f"s_x1_store{i}") for i in range(NX)]

        with ExitStack() as p1:
            w_hi = {w: sb(p1, f"w{w}_hi", [P, DC, D], F32R) for w in "qkvo"}
            w_lo = {w: sb(p1, f"w{w}_lo", [P, DC, D], F32R) for w in "qkvo"}
            ws_sb = sb(p1, "ws_sb", [P, DC, QUAD])
            bs_b = sb(p1, "bs_b", [P, E])
            bo_b = sb(p1, "bo_b", [P, D])
            ones = sb(p1, "ones", [P, QUAD])
            bias_cols = sb(p1, "bias_cols", [P, 3 * DC])
            half = sb(p1, "half", [P, 1])
            keep_scale = sb(p1, "keep_scale", [P, B])
            xT = [sb(p1, f"xT_{k}", [P, DC, S], F32R) for k in ("hi", "lo")]
            cT = [sb(p1, f"cT_{k}", [P, DC, SK], F32R) for k in ("hi", "lo")]
            qk = {(w, k): sb(p1, f"{w}T_{k}", [P, S], F32R) for w in "qk" for k in ("hi", "lo")}
            NST = 3
            kst = [sb(p1, f"kst{i}", [P, HG, SK], F32R) for i in range(NST)]
            qst = [sb(p1, f"qst{i}", [P, HG, S], F32R) for i in range(NST)]
            ROW_MASK, ROWS_MAX, ROWS_ALL = 3 * DH, 3 * DH + 1, 3 * DH + 3
            v_sb = sb(p1, "v_sb", [P, KT, D])
            NP_ = 6
            p_ring = [sb(p1, f"p_ring{i}", [P, S]) for i in range(NP_)]
            x_in = [sb(p1, f"x_in{i}", [P, D]) for i in range(NX)]
            maxes = sb(p1, "maxes", [P, HG * TB])
            nmax = [sb(p1, f"nmax_{k}", [HG * TB, P], F32R) for k in ("hi", "lo")]
            rden = sb(p1, "rden", [P, S])
            att_n = sb(p1, "att_n", [P, S])
            oT = [sb(p1, f"oT_{k}", [P, GB, S], F32R) for k in ("hi", "lo")]
            hnT = sb(p1, "hnT", [P, DC, P])
            stat = [sb(p1, f"stat{i}", [P, 6]) for i in range(2)]
            mv = [sb(p1, f"mv{i}", [P, 2]) for i in range(2)]
            rstd = [sb(p1, f"rstd{i}", [P, 1]) for i in range(2)]
            rt_max = sb(p1, "rt_max", [P, TB])
            rt_sum = sb(p1, "rt_sum", [P, TB])

            ones_b = hnT[0:B, 0, :]
            mask_u8 = hnT[0:B, 1, :].bitcast(U8)
            bias_rows = hnT[0:3 * DC, 2, :]
            mask_neg = rden[0:B, :]

            x_in_free = [[] for _ in range(NX)]
            s_x_in = [sem(f"s_x_in{i}") for i in range(NX)]
            x_turn = [0]
            t_xT_read, t_cT_read = [], []
            s_ln = sem("s_ln")
            s_rs = sem("s_rs")
            s_norm = sem("s_norm")
            ln_turn = [0]
            ln_free = [[], []]

            def layernorm(src, dst, t_src, dst_free, then):
                i = ln_turn[0] % 2
                ln_turn[0] += 1
                t = put("dve", t_src + ln_free[i], lambda e: e.bn_stats(stat[i][:, :], src), s_ln)
                t_mv = put("dve", [t], lambda e: e.bn_aggr(mv[i][:, :], stat[i][:, :]), s_ln)
                t = put("dve", [t_mv], lambda e: e.tensor_scalar(rstd[i][:, :], mv[i][:, 1:2], EPS, None, ALU.add), s_ln)
                t = put("pool", [t, (s_const, s_const.count)], lambda e: e.tensor_tensor(rstd[i][:, :], rstd[i][:, :], half[:, :], ALU.pow), s_rs)

                def normalise():
                    tn = put("dve", [t] + dst_free(), lambda e: e.tensor_scalar(
                        dst, src, mv[i][:, 0:1], rstd[i][:, 0:1], ALU.subtract, ALU.mult), s_norm)
                    ln_free[i] = [tn]
                    then(tn)
                return normalise

            def store_split(bank, dst, view, bias, t_full, waits, stored, lo_waits=()):
                if bias is None:
                    t_hi = put("act", [t_full] + waits, lambda e: e.activation(dst[0], view, ACT.Copy), s_ev_act)
                else:
                    t_hi = put("act", [t_full, t_bias] + waits, lambda e: e.activation(
                        dst[0], view, ACT.Identity, bias=bias), s_ev_act)

                def lo():
                    w = [t_full, t_hi, *lo_waits] + waits
                    if bias is None:
                        t_lo = put("dve", w, lambda e: e.tensor_tensor(dst[1], view, raw(dst[0]), ALU.subtract), s_ev_dve)
                    else:
                        t_lo = put("dve", w, lambda e: e.scalar_tensor_tensor(
                            dst[1], view, bias, raw(dst[0]), ALU.add, ALU.subtract), s_ev_dve)
                    gen_free[bank] = [t_hi, t_lo]
                    gen_late.discard(bank)
                    stored(t_hi, t_lo)
                gen_late.add(bank)
                deferred.append(lo)

            t_tr = {}
            loaded = {}

            s_first_in = {kind: [sem(f"s_first_{kind}{i}") for i in range(TB)] for kind in "xc"}

            def tile_in(kind, b, slot):
                return v_sb[:, slot, :] if (kind, b) == ("c", 0) else x_in[slot][:, :]

            def load_tile(kind, b, t):
                src = (x_tok if kind == "x" else ctx_tok)[(b * TB + t) * P:(b * TB + t + 1) * P, :]
                if b == 0:
                    slot = t
                    tk = put("sp", [], lambda e: e.dma_start(tile_in(kind, b, slot), src), s_first_in[kind][t], 16)
                else:
                    slot = x_turn[0] % NX
                    x_turn[0] += 1
                    tk = put("pool", x_in_free[slot], lambda e: e.dma_start(x_in[slot][:, :], src), s_x_in[slot], 16)
                loaded[kind, b, t] = (slot, tk)

            def normalise_tile(b, t):
                slot, tk = loaded["x", b, t]
                deferred.append(layernorm(x_in[slot][:, :], x_in[slot][:, :], [tk], lambda: [],
                                          lambda tn: loaded.update({("x", b, t): (slot, tn)})))

            def transpose_tile(kind, b, t):
                slot, tk = loaded[kind, b, t]
                dst = xT if kind == "x" else cT
                bank, free = take_bank()
                tile = tile_in(kind, b, slot)

                def run(e):
                    for c in range(DC):
                        last = e.transpose(ps_gen[bank][:, c * P:(c + 1) * P], tile[:, c * P:(c + 1) * P], ident[:, :])
                    return last
                tf = put("pe", free + [tk, t_ident], run, s_gen)
                if (kind, b) != ("c", 0):
                    x_in_free[slot] = [tf]
                view = ps_gen[bank][:, :].rearrange("p (c t) -> p c t", c=DC)
                cols = [d[:, :, t * P:(t + 1) * P] for d in dst]
                old = t_xT_read if kind == "x" else t_cT_read
                store_split(bank, cols, view, None, tf, list(old),
                            lambda t_hi, t_lo: t_tr.setdefault((kind, b), []).extend([t_hi, t_lo]))

            put("pool", [], lambda e: e.memset(ones[:, :], 1.0), s_const)
            put("pool", [], lambda e: e.memset(half[:, :], -0.5), s_const)
            t_const = (s_const, s_const.count)

            s_w_in = [sem(f"s_w_in{i}") for i in range(NP_)]
            s_w_hi, s_w_lo = sem("s_w_hi"), sem("s_w_lo")
            stage_free = [[] for _ in range(NP_)]
            t_w, staged = {}, [0]

            def split_weight(w, c, stage, t_in):
                t_hi = put("act", [t_in], lambda e: e.activation(w_hi[w][:, c, :], stage[:, :], ACT.Copy), s_w_hi)
                t_lo = put("dve", [t_in, t_hi], lambda e: e.tensor_tensor(
                    w_lo[w][:, c, :], stage[:, :], raw(w_hi[w][:, c, :]), ALU.subtract), s_w_lo)
                t_w[w] = [t_hi, t_lo]
                return [t_hi, t_lo]

            def load_weight(w, src):
                def chunk(c):
                    slot = staged[0] % NP_
                    staged[0] += 1
                    t_in = put("sp", stage_free[slot], lambda e: e.dma_start(
                        p_ring[slot][:, :], src[c * P:(c + 1) * P, :]), s_w_in[slot], 16)

                    def split():
                        stage_free[slot] = split_weight(w, c, p_ring[slot], t_in)
                    return split
                return [chunk(c) for c in range(DC)]

            def load_wo(c):
                slot = x_turn[0] % NX
                x_turn[0] += 1
                t_in = put("pool", x_in_free[slot], lambda e: e.dma_start(
                    x_in[slot][:, :], Wo[c * P:(c + 1) * P, :]), s_x_in[slot], 16)
                wo_steps.append(lambda: x_in_free.__setitem__(slot, split_weight("o", c, x_in[slot], t_in)))

            wo_steps = []

            for kind in "xc":
                for t in range(TB):
                    load_tile(kind, 0, t)
            for t in range(TB):
                normalise_tile(0, t)
                transpose_tile("c", 0, t)
                flush()
                transpose_tile("x", 0, t)
            flush()
            t_ones_rows = {}

            def ones_rows(i):
                for rows in (kst[i], qst[i]):
                    t_ones_rows[i] = put("pool", [(s_const, s_const.count), (s_rs, s_rs.count)], lambda e, rows=rows: e.memset(raw(rows[ROW_MASK:P, :, :]), 1.0), s_const)
            ones_rows(0)

            put("sp", [], lambda e: e.dma_start(ws_sb[:, :, 0:E], Ws.rearrange("(c p) n -> p c n", p=P)), s_bias_in, 16)
            put("sp", [], lambda e: e.dma_start(bs_b[:, :], bs.rearrange("(a n) -> a n", a=1).to_broadcast([P, E])), s_bias_in, 16)
            put("sp", [], lambda e: e.dma_start(bo_b[:, :], bo.rearrange("(a n) -> a n", a=1).to_broadcast([P, D])), s_bias_in, 16)
            for n, v in enumerate((bq, bk, bv)):
                put("sp", [], lambda e, n=n, v=v: e.dma_start(
                    bias_rows[n * DC:(n + 1) * DC, :], v.rearrange("(c p) -> c p", p=P)), s_bias_in, 16)
            put("sp", [], lambda e: e.dma_start(mask_u8, mask), s_bias_in, 16)
            t_bias_in = (s_bias_in, s_bias_in.count)
            wk_steps = load_weight("k", Wk)
            t_ws0 = put("pool", [(s_const, s_const.count)], lambda e: e.memset(ws_sb[:, :, E:QUAD], 0.0), s_const)

            s_mask = sem("s_mask")
            t = put("dve", [t_bias_in], lambda e: e.tensor_scalar(
                mask_neg, mask_u8, 1.0, MASKED, ALU.subtract, ALU.mult), s_mask)
            s_mask_store = sem("s_mask_store")
            t_mask = put("sp", [t], lambda e: e.dma_start(raw(mask_rows), mask_neg), s_mask_store, 16)

            mask_any = sb(p1, "mask_any", [B, 1])
            mask_diag = sb(p1, "mask_diag", [B, B])
            s_any = sem("s_any")
            t_ones_b = put("dve", [], lambda e: e.memset(ones_b, SCALE), s_any)
            t_any = put("dve", [t_bias_in], lambda e: e.reduce_max(mask_any[:, :], mask_u8, AX.X), s_any)
            t_any = put("dve", [t_any, t_ident], lambda e: e.tensor_scalar(
                mask_diag[:, :], ident[0:B, 0:B], mask_any[:, 0:1], None, ALU.mult), s_any)
            bank, free = take_bank()
            t = put("pe", free + [t_any, t_ones_b], lambda e, bank=bank: e.matmul(
                ps_gen[bank][:, 0:B], lhsT=ones_b, rhs=mask_diag[:, :], start=True, stop=True), s_gen)
            t_keep = put("dve", [t], lambda e, bank=bank: e.tensor_copy(keep_scale[:, :], ps_gen[bank][:, 0:B]), s_ev_dve)
            gen_free[bank] = [t_keep]
            bank, free = take_bank()
            t = put("pe", free + [t_bias_in, t_ident], lambda e, bank=bank: e.transpose(
                ps_gen[bank][:, 0:3 * DC], bias_rows, ident[0:3 * DC, 0:3 * DC]), s_gen)
            t_bias = put("dve", [t], lambda e, bank=bank: e.tensor_copy(bias_cols[:, :], ps_gen[bank][:, 0:3 * DC]), s_ev_dve)
            gen_free[bank] = [t_bias]

            for step in wk_steps:
                step()
            for step in load_weight("q", Wq):
                step()

            v_free = []
            t_v = {}

            def project_v(b, t):
                bank, free = take_bank()
                cols = slice(t * P, (t + 1) * P)

                tf = put("pe", free + t_tr["c", b] + t_w["v"], lambda e: three(
                    ps_gen[bank][:, :], [((cT[0][:, c, cols], cT[1][:, c, cols]),
                                          (w_hi["v"][:, c, :], w_lo["v"][:, c, :])) for c in range(DC)], e), s_gen)
                t_cT_read[:] = [tf]
                tv = put("act", [tf] + v_free, lambda e: e.activation(v_sb[:, t, :], ps_gen[bank][:, :], ACT.Copy), s_ev_act)
                gen_free[bank] = [tv]
                t_v[b] = tv

            s_stack = [{w: sem(f"s_stack_{w}{i}") for w in "qk"} for i in range(NST)]
            s_mask_row = [sem(f"s_mask_row{i}") for i in range(NST)]
            mask_of, t_mask_row = [None] * NST, [None] * NST
            stack_free = [[] for _ in range(NST)]
            t_stack = {}
            qk_free = {(w, k): [] for w in "qk" for k in ("hi", "lo")}
            s_stack_lo = [{w: sem(f"s_stack_lo_{w}{i}") for w in "qk"} for i in range(NST)]

            def project_qk(w, g):
                b, c4 = divmod(g, GB)
                k = g % NST
                src = xT if w == "q" else cT
                dst = qst[k] if w == "q" else kst[k]
                cols = slice(c4 * P, (c4 + 1) * P)
                held = {}

                def begin():
                    held["bank"], free = take_bank()
                    gen_open.add(held["bank"])
                    return free

                def finish(tf):
                    bank = held["bank"]
                    gen_open.discard(bank)
                    gen_order.remove(bank)
                    gen_order.append(bank)
                    (t_xT_read if w == "q" else t_cT_read)[:] = [tf]
                    n = ("q", "k").index(w) * DC + c4
                    store_split(bank, [qk[w, "hi"][:, :], qk[w, "lo"][:, :]], ps_gen[bank][:, :],
                                bias_cols[:, n:n + 1], tf, qk_free[w, "hi"], stack, qk_free[w, "lo"])

                def stack(*parts):
                    order = ("hi", "lo", "hi") if w == "q" else ("hi", "hi", "lo")
                    sems = {"hi": s_stack[k][w], "lo": s_stack_lo[k][w]}
                    for part in ("hi", "lo"):
                        for h in range(HG):
                            for r in range(3):
                                if order[r] != part:
                                    continue
                                put("pool" if w == "k" else "sp", [parts[("hi", "lo").index(part)], t_ones_rows[k]] + stack_free[k],
                                    lambda e, h=h, r=r, part=part: e.dma_start(
                                        raw(dst[r * DH:(r + 1) * DH, h, :]), raw(qk[w, part][h * DH:(h + 1) * DH, :])), sems[part], 16)
                    t_hi_out, t_lo_out = [(sm, sm.count) for sm in sems.values()]
                    qk_free[w, "hi"], qk_free[w, "lo"] = [t_hi_out, parts[1]], [t_lo_out]
                    if w == "k" and mask_of[k] != b:
                        mask_of[k] = b
                        src_m = raw(mask_rows[b:b + 1, :]).rearrange("p (a n) -> p a n", a=1).to_broadcast([1, HG, SK])
                        t_mask_row[k] = put("sp", [t_mask, t_ones_rows[k]] + stack_free[k], lambda e: e.dma_start(
                            raw(kst[k][ROW_MASK:ROW_MASK + 1, :, :]), src_m), s_mask_row[k], 16)
                    if w == "k":
                        t_stack["mask", g] = t_mask_row[k]
                    t_stack[w, g] = [t_hi_out, t_lo_out]

                def part(i):
                    free = begin() if i == 0 else []
                    wh, wl = w_hi[w][:, i, cols], w_lo[w][:, i, cols]
                    mh, ml = src[0][:, i, :], src[1][:, i, :]
                    psum = ps_gen[held["bank"]][:, :]

                    def run(e):
                        e.matmul(psum, lhsT=wh, rhs=mh, start=(i == 0), stop=False)
                        e.matmul(psum, lhsT=wh, rhs=ml, start=False, stop=False)
                        return e.matmul(psum, lhsT=wl, rhs=mh, start=False, stop=(i == DC - 1))
                    tiles = t_tr["x" if w == "q" else "c", b]
                    assert len(tiles) == 2 * TB
                    waits = free + tiles + t_w[w] if i == 0 else []
                    tf = put("pe", waits, run, s_gen)
                    if i == DC - 1:
                        finish(tf)
                return [lambda i=i: part(i) for i in range(DC)]

            s_max = sem("s_max")
            s_maxrow = [sem(f"s_maxrow{i}") for i in range(NST)]
            t_maxrow = {}
            maxes_free, nmax_free = [], []
            last_max = []

            def row_max(g, h, t):
                bank, free = take_bank()
                ks, qs = kst[g % NST], qst[g % NST]
                tf = put("pe", free + t_stack["q", g] + t_stack["k", g] + [t_stack["mask", g]], lambda e: e.matmul(
                    ps_gen[bank][:, :], lhsT=qs[0:ROWS_MAX, h, t * P:(t + 1) * P], rhs=ks[0:ROWS_MAX, h, :],
                    start=True, stop=True), s_gen)
                col = h * TB + t
                tm = put("dve", [tf] + maxes_free, lambda e: e.reduce_max(maxes[:, col:col + 1], ps_gen[bank][:, :], AX.X), s_max)
                gen_free[bank] = [tm]
                if (h, t) == (HG - 1, TB - 1):
                    last_max.append((tf, tm))

            def max_rows(g):
                tf, tm = last_max.pop()
                bank, free = take_bank()
                tt = put("pe", free + [tm, t_ident], lambda e: e.transpose(
                    ps_gen[bank][0:HG * TB, 0:P], maxes[:, :], ident[:, :]), s_gen)
                maxes_free[:] = [tt]
                view = ps_gen[bank][0:HG * TB, 0:P]
                t_hi = put("act", [tt] + nmax_free, lambda e: e.activation(nmax[0][:, :], view, ACT.Copy, scale=-1.0), s_ev_act)

                def lo():
                    t_lo = put("dve", [tt, t_hi] + nmax_free, lambda e: e.scalar_tensor_tensor(
                        nmax[1][:, :], view, -1.0, raw(nmax[0][:, :]), ALU.mult, ALU.subtract), s_ev_dve)
                    gen_free[bank] = [t_hi, t_lo]
                    gen_late.discard(bank)
                    sm = s_maxrow[g % NST]
                    for r in range(2):
                        row = ROWS_MAX + r
                        dst = qst[g % NST][row:row + 1, :, :].rearrange("p h (t n) -> p (h t) n", n=P)
                        put("pool", [t_hi, t_lo, tf], lambda e, r=r, dst=dst: e.dma_start(raw(dst), raw(nmax[r][:, :])), sm, 16)
                    nmax_free[:] = [(sm, sm.count)]
                    t_maxrow[g] = (sm, sm.count)
                gen_late.add(bank)
                deferred.append(lo)

            s_st, s_exp, s_av = sem("s_st"), sem("s_exp"), sem("s_av")
            p_free = [[] for _ in range(NP_)]
            p_slot = {}
            sc_turn = [0]

            def scores(g, kt, h):
                ks, qs = kst[g % NST], qst[g % NST]
                slot = sc_turn[0] % NP_
                bank, free = take_bank()
                sc_turn[0] += 1
                ts = put("pe", free + [t_maxrow[g]], lambda e: e.matmul(
                    ps_gen[bank][:, :], lhsT=ks[0:ROWS_ALL, h, kt * P:(kt + 1) * P], rhs=qs[0:ROWS_ALL, h, :],
                    start=True, stop=True), s_st)
                if kt == KT - 1:
                    stack_free[g % NST] = [ts]
                b = g // GB
                te = put("act", [ts, t_keep] + p_free[slot], lambda e: e.activation(
                    p_ring[slot][:, :], ps_gen[bank][:, :], ACT.Exp, scale=keep_scale[:, b:b + 1]), s_exp)
                gen_free[bank] = [te]
                p_slot[g, kt, h] = (slot, te)

            att_free = []
            t_oT = {}
            oT_free = []
            s_nrm, s_oh, s_ol = sem("s_nrm"), sem("s_oh"), sem("s_ol")
            s_rd = sem("s_rd")
            soon = []
            nrm_free = [t_mask, t_bias, t_keep]

            def attend(g, kt, psum):
                b, c4 = divmod(g, GB)
                slots = [p_slot[g, kt, h] for h in range(HG)]

                def run(e):
                    for h in range(HG):
                        w = v_sb[:, kt, (c4 * HG + h) * DH:(c4 * HG + h + 1) * DH] if psum is ps_att else ones[:, :]
                        last = e.matmul(psum[h * DH:(h + 1) * DH, :], lhsT=w, rhs=p_ring[slots[h][0]][:, :],
                                        start=(kt == 0), stop=(kt == KT - 1))
                    return last
                ta = put("pe", [s[1] for s in slots] + [t_v[b], t_const] + (list(att_free) if kt == 0 else []), run, s_av)
                for s in slots:
                    p_free[s[0]] = [ta]
                if psum is ps_att:
                    return
                if kt < KT - 1:
                    return
                if c4 == GB - 1:
                    v_free[:] = [ta]
                tc = put("act", [ta] + nrm_free, lambda e: e.activation(rden[:, :], ps_den[:, :], ACT.Copy), s_nrm)
                ta = put("act", [ta] + nrm_free, lambda e: e.activation(att_n[:, :], ps_att[:, :], ACT.Copy), s_nrm)
                att_free[:] = [ta]
                tr = []

                def quarter(n):
                    c = slice(n * P, (n + 1) * P)
                    t = put("dve", [tc], lambda e: e.reciprocal(rden[:, c], rden[:, c]), s_rd)
                    tr[:] = [t]

                def divide():
                    tr[:] = [put("dve", [ta] + tr, lambda e: e.tensor_tensor(att_n[:, :], att_n[:, :], rden[:, :], ALU.mult), s_rd)]

                def split_output():
                    tn = tr[0]
                    bias = bias_cols[:, 2 * DC + c4:2 * DC + c4 + 1]
                    free = list(oT_free)
                    th = put("act", [tn, t_bias] + free, lambda e: e.activation(
                        oT[0][:, c4, :], att_n[:, :], ACT.Identity, bias=bias), s_oh)

                    def lo():
                        tl = put("dve", [tn, th] + free, lambda e: e.scalar_tensor_tensor(
                            oT[1][:, c4, :], att_n[:, :], bias, raw(oT[0][:, c4, :]), ALU.add, ALU.subtract), s_ol)
                        nrm_free[:] = [th, tl]
                        t_oT[b, c4] = [th, tl]
                    deferred.append(lo)
                soon.extend([lambda n=n: quarter(n) for n in range(S // P)] + [divide, lambda: None, split_output])

            s_x1 = sem("s_x1")
            t_hn = {}

            residual, x1_normal = {}, {}

            def normalise_x1(b, t):
                x1_normal.pop(b * TB + t)()

            def load_residual(b, t):
                rows = slice((b * TB + t) * P, (b * TB + t + 1) * P)
                xs = x_turn[0] % NX
                x_turn[0] += 1
                tr = put("pool", x_in_free[xs], lambda e: e.dma_start(x_in[xs][:, :], x_tok[rows, :]), s_x_in[xs], 16)
                residual[b, t] = (xs, tr)

            def add_bias(b, t):
                xs, tr = residual[b, t]
                tr = put("pool", [tr, t_bias_in], lambda e: e.tensor_tensor(x_in[xs][:, :], x_in[xs][:, :], bo_b[:, :], ALU.add), s_x1)
                residual[b, t] = (xs, tr)

            held_out = {}

            def output_sum(b, t, chunks):
                if chunks[0] == 0:
                    held_out[b, t] = take_bank()
                    gen_open.add(held_out[b, t][0])
                bank, free = held_out[b, t]
                cols = slice(t * P, (t + 1) * P)

                def run(e):
                    for c in chunks:
                        oh, ol = oT[0][:, c, cols], oT[1][:, c, cols]
                        wh, wl = w_hi["o"][:, c, :], w_lo["o"][:, c, :]
                        e.matmul(ps_gen[bank][:, :], lhsT=oh, rhs=wh, start=(c == 0), stop=False)
                        e.matmul(ps_gen[bank][:, :], lhsT=oh, rhs=wl, start=False, stop=False)
                        last = e.matmul(ps_gen[bank][:, :], lhsT=ol, rhs=wh, start=False, stop=(c == GB - 1))
                    return last
                return put("pe", free + t_oT[b, chunks[-1]] + t_w["o"], run, s_gen)

            def output_tile(b, t, chunks=tuple(range(GB))):
                n = b * TB + t
                rows = slice(n * P, (n + 1) * P)
                xs, tr = residual[b, t]
                x1 = x_in[xs]
                tf = output_sum(b, t, chunks)
                bank, _ = held_out[b, t]
                gen_open.discard(bank)
                oT_free[:] = [tf]
                t1 = put("dve", [tf, tr], lambda e: e.tensor_tensor(
                    x1[:, :], ps_gen[bank][:, :], x1[:, :], ALU.add), s_ev_dve)
                gen_free[bank] = [t1]
                ts = put("sp", [t1], lambda e: e.dma_start(out_tok[rows, :], x1[:, :]), s_x1_store[xs], 16)

                def store_row(th):
                    tsh = put("sp", [th], lambda e: e.dma_start(hn_rows[rows, 0:D], x1[:, :]), s_hn_store[xs], 16)
                    t_hn[n] = (xs, th, tsh)
                x1_normal[n] = layernorm(x1[:, :], x1[:, :], [t1], lambda: [ts], store_row)

            s_hnT, s_lg = sem("s_hnT"), sem("s_lg")
            hnT_free, held_lg = [], {}

            held_hnT = {}

            def hnT_of(n):
                return hnT if n < NT - TB else v_sb[:, n - (NT - TB), :].rearrange("p (c t) -> p c t", c=DC)

            def route_tile(b, t):
                n = b * TB + t
                slot, th, tsh = t_hn[n]
                bank, free = take_bank()

                def run(e):
                    for c in range(DC):
                        last = e.transpose(ps_gen[bank][:, c * P:(c + 1) * P], x_in[slot][:, c * P:(c + 1) * P], ident[:, :])
                    return last
                tf = put("pe", free + [th], run, s_gen)
                x_in_free[slot] = [tf, tsh]
                own = hnT_of(n)
                tc = put("act", [tf] + (hnT_free if own is hnT else v_free), lambda e: e.activation(
                    own[:, :, :], ps_gen[bank][:, :].rearrange("p (c t) -> p c t", c=DC), ACT.Copy), s_ev_act)
                gen_free[bank] = [tc]
                held_hnT[n] = tc

            def logits_tile(b, t):
                n = b * TB + t
                bank, free = take_bank()
                own = hnT_of(n)

                def run(e):
                    for c in range(DC):
                        last = e.matmul(ps_gen[bank][c * QUAD:(c + 1) * QUAD, 0:P], lhsT=ws_sb[:, c, :], rhs=own[:, c, :],
                                        start=True, stop=True)
                    return last
                tf = put("pe", free + [held_hnT[n], t_bias_in, t_ws0], run, s_gen)
                lgT = own[:, 0, :]
                held_lg[n] = put("act", [tf], lambda e: e.activation(
                    lgT, ps_gen[bank][:, 0:P], ACT.Copy), s_ev_act)
                gen_free[bank] = [held_lg[n]]

            def logits_back(b, t):
                n = b * TB + t
                bank, free = take_bank()
                tf = put("pe", free + [held_lg[n]], lambda e: e.transpose(ps_gen[bank][:, 0:P], hnT_of(n)[:, 0, :], ident[:, :]), s_gen)
                hnT_free[:] = [tf]
                parts = ps_gen[bank][:, 0:P].rearrange("p (c w) -> p w c", w=QUAD)[:, 0:E, :]
                ts = put("dve", [tf], lambda e: e.reduce_sum(probs[:, n, :], parts, AX.X), s_ev_dve)
                gen_free[bank] = [ts]
                tl = put("dve", [ts], lambda e: e.tensor_tensor(probs[:, n, :], probs[:, n, :], bs_b[:, :], ALU.add), s_lg)
                if t == TB - 1:
                    softmax_rows(b, tl)

            def softmax_rows(b, t):
                v = probs[:, b * TB:(b + 1) * TB, :]
                def wide(a):
                    return a[:, :].rearrange("p (t a) -> p t a", a=1).to_broadcast([P, TB, E])
                t = put("dve", [t], lambda e: e.reduce_max(rt_max[:, :], v, AX.X), s_lg)
                t = put("dve", [t], lambda e: e.tensor_tensor(v, v, wide(rt_max), ALU.subtract), s_lg)
                t = put("act", [t], lambda e: e.activation(v, v, ACT.Exp), s_hnT)
                t = put("dve", [t], lambda e: e.reduce_sum(rt_sum[:, :], v, AX.X), s_lg)
                t = put("dve", [t], lambda e: e.reciprocal(rt_sum[:, :], rt_sum[:, :]), s_lg)
                t = put("dve", [t], lambda e: e.tensor_tensor(v, v, wide(rt_sum), ALU.mult), s_lg)
                rows = hn_rows[b * S:(b + 1) * S, D:D + E].rearrange("(t p) e -> p t e", p=P)
                put("sp", [t], lambda e: e.dma_start(rows, v), s_probs_store, 16)
                return t

            GAPS = 5 * KT
            places = []

            def each(f, *args):
                return [lambda t=t: f(*args, t) for t in range(TB)]

            K_AT = ((-0.08, 0.13), (0.08, 0.22), (0.03, 0.22), (0.08, 0.25))
            Q_AT = ((0.33, 0.45), (0.23, 0.42), (0.29, 0.45), (0.23, 0.47))
            MAX_AT = ((-0.02, 0.68), (-0.18, 0.65), (-0.1, 0.71), (0.0, 0.71))
            ROWS_AT = (0.72, 0.72, 0.72, 0.72)
            V_AT = (0.13, 0.33)
            LOAD_C_AT, TURN_C_AT = (-0.1, 0.22), (0.5, 0.95)
            LOAD_X_AT, NORM_X_AT, TURN_X_AT = (0.6, 0.95), (0.75, 1.12), (0.97, 1.16)
            LATE_AT = ((load_residual, 0.15), (add_bias, 0.38), (output_tile, 0.5), (normalise_x1, 0.61),
                       (route_tile, 0.7), (logits_tile, 0.75), (logits_back, 0.8))
            LATE_FOR = 0.52

            def place(start, span, steps):
                a, b = start + span[0], start + span[1]
                for k, step in enumerate(steps):
                    places.append((a + (b - a) * (k + 0.5) / len(steps), step))

            for i in range(NG):
                r, b = i % GB, i // GB
                if i + 2 < NG:
                    place(i, K_AT[r], project_qk("k", i + 2))
                    place(i, Q_AT[r], project_qk("q", i + 2))
                if i + 1 < NG:
                    place(i, MAX_AT[r], [lambda h=h, t=t, g=i + 1: row_max(g, h, t) for h in range(HG) for t in range(TB)])
                    place(i, (ROWS_AT[r], ROWS_AT[r]), [lambda g=i + 1: max_rows(g)])
                if r == 0:
                    place(i, V_AT, each(project_v, b))
                    if b > 0:
                        for step, at in LATE_AT:
                            place(i, (at, at + LATE_FOR), each(step, b - 1))
                if r == 1 and b + 1 < B:
                    place(i, LOAD_C_AT, each(load_tile, "c", b + 1))
                    place(i, TURN_C_AT, each(transpose_tile, "c", b + 1))
                    place(i, LOAD_X_AT, each(load_tile, "x", b + 1))
                    place(i, NORM_X_AT, each(normalise_tile, b + 1))
                    place(i, TURN_X_AT, each(transpose_tile, "x", b + 1))
            place(0, (0.0, 0.3), [lambda c=c: load_wo(c) for c in range(DC)])
            place(0, (0.4, 0.85), [lambda c=c: wo_steps[c]() for c in range(DC)])
            places.sort(key=lambda p: p[0])

            wv_steps = load_weight("v", Wv)
            for step in (project_qk("k", 0) + project_qk("q", 0) + [lambda: ones_rows(1), lambda: ones_rows(2)]
                         + project_qk("k", 1) + project_qk("q", 1)):
                step()
                flush()
            for h in range(HG):
                for t in range(TB):
                    row_max(0, h, t)
                wv_steps[h]()
            max_rows(0)
            flush()

            def fill(time):
                flush()
                if soon:
                    soon.pop(0)()
                while places and places[0][0] < time:
                    places.pop(0)[1]()

            for i in range(NG):
                for kt in range(KT):
                    before = (i, kt - 1) if kt else (i - 1, KT - 1)
                    time = [i + (5 * kt + n) / GAPS for n in range(1, 6)]
                    scores(i, kt, 0)
                    scores(i, kt, 1)
                    fill(time[0])
                    if before[0] >= 0:
                        attend(*before, ps_att)
                    fill(time[1])
                    if before[0] >= 0:
                        attend(*before, ps_den)
                    scores(i, kt, 2)
                    fill(time[2])
                    scores(i, kt, 3)
                    fill(time[3])
                    fill(time[4])
                flush()
            for t in range(TB):
                load_residual(B - 1, t)
            for t in range(TB):
                add_bias(B - 1, t)
            attend(NG - 1, KT - 1, ps_att)
            attend(NG - 1, KT - 1, ps_den)
            for t in range(TB):
                output_sum(B - 1, t, tuple(range(GB - 1)))
            while soon:
                soon.pop(0)()
            flush()
            for t in range(TB):
                output_tile(B - 1, t, (GB - 1,))
                if t % 2:
                    for k in (t - 1, t):
                        normalise_x1(B - 1, k)
                        route_tile(B - 1, k)
            for f in (logits_tile, logits_back):
                for t in range(TB):
                    f(B - 1, t)
            t_x1_all = [(s, s.count) for s in s_x1_store]
            t_hn_all = [(s, s.count) for s in (*s_hn_store, s_probs_store)]
            t_part1 = [(s, s.count) for s in (s_gen, s_st, s_av, s_ev_act, s_ev_dve, s_exp, s_oh, s_ol, s_nrm, s_rd,
                                              s_norm, s_hnT, s_lg, s_x1)] + t_x1_all + t_hn_all

        FB = 2 * P
        NPIECE = F // FB
        NF = F // P
        TT = K // P
        with ExitStack() as p3:
            NR, NS = 3, 3
            idx = sb(p3, "idx", [P, E, TT], I32)
            w1_raw = [sb(p3, f"w1_raw{i}", [P, DC, FB]) for i in range(NR)]
            w2_raw = [sb(p3, f"w2_raw{i}", [P, 2, D]) for i in range(NR)]
            w1s = [[sb(p3, f"w1_{k}{i}", [P, DC, FB], F32R) for k in ("hi", "lo")] for i in range(NS)]
            w2s = [[sb(p3, f"w2_{k}{i}", [P, 2, D], F32R) for k in ("hi", "lo")] for i in range(NS)]
            rows = [sb(p3, f"rows{i}", [P, ROW]) for i in range(2 * TT)]
            b1_raw = sb(p3, "b1_raw", [P, P])
            b1_cols = sb(p3, "b1_cols", [P, P])

            s_w1_in = [sem(f"s_w1_in{i}") for i in range(NR)]
            s_w2_in = [sem(f"s_w2_in{i}") for i in range(NR)]
            s_split, s_split_act, s_split_pool = sem("s_split"), sem("s_split_act"), sem("s_split_pool")
            raw_free = [[] for _ in range(NR)]
            split_free = [[[], []] for _ in range(NS)]
            pieces = [(e, j) for e in range(E) for j in range(NPIECE)]
            t_in, t_sp = {}, {}

            def load_piece(n):
                ex, j = pieces[n]
                r = n % NR
                w1v = W1[ex, :, j * FB:(j + 1) * FB].rearrange("(c p) f -> p c f", p=P)
                w2v = W2[ex, j * FB:(j + 1) * FB, :].rearrange("(c p) d -> p c d", p=P)
                ta = put("sp", raw_free[r], lambda e: e.dma_start(w1_raw[r][:, :, :], w1v), s_w1_in[r], 16)
                tb = put("sp", raw_free[r], lambda e: e.dma_start(w2_raw[r][:, :, :], w2v), s_w2_in[r], 16)
                t_in[n] = (ta, tb)

            def split_early(n):
                got = []
                for k, (rw, sp_) in enumerate(((w1_raw[n], w1s[n]), (w2_raw[n], w2s[n]))):
                    th = put("act", [t_in[n][k]] + t_part1, lambda e, rw=rw, sp_=sp_: e.activation(
                        sp_[0][:, :, :], rw[:, :, :], ACT.Copy), s_split_act)
                    tl = put("pool", [th], lambda e, rw=rw, sp_=sp_: e.tensor_tensor(
                        sp_[1][:, :, :], rw[:, :, :], raw(sp_[0][:, :, :]), ALU.subtract), s_split_pool)
                    got.append(tl)
                raw_free[n] = [tl]
                t_sp[n] = got

            def split_piece(n):
                r, s = n % NR, n % NS
                got = []
                for k, (rw, sp_) in enumerate(((w1_raw[r], w1s[s]), (w2_raw[r], w2s[s]))):
                    th = put("dve", [t_in[n][k]] + split_free[s][k], lambda e, rw=rw, sp_=sp_: e.tensor_copy(
                        sp_[0][:, :, :], rw[:, :, :]), s_split)
                    tl = put("dve", [th], lambda e, rw=rw, sp_=sp_: e.tensor_tensor(
                        sp_[1][:, :, :], rw[:, :, :], raw(sp_[0][:, :, :]), ALU.subtract), s_split)
                    got.append(tl)
                raw_free[r] = [tl]
                t_sp[n] = got

            q.steps["sp"].append((t_part1, lambda e: None, None, 0))
            for n in range(NR):
                load_piece(n)

            HALF = E // 2
            A_N, B_N = QUAD, K // QUAD
            TOK0 = N // 2
            STEP_BITS = 2
            SHIFTS = range(30 - STEP_BITS, -1, -STEP_BITS)
            NCAND = 1 << STEP_BITS
            s_c2, s_sel, s_cnt, s_tot2 = sem("s_c2"), sem("s_sel"), sem("s_cnt"), sem("s_tot2")
            p2 = ExitStack()
            pT = sb(p2, "pT", [P, 2 * P])
            expert_of = sb(p2, "expert_of", [P, E])
            same = sb(p2, "same", [P, P])
            tri = sb(p2, "tri", [P, P], BF16)
            ones_h = sb(p2, "ones_h", [P, P], BF16)
            ones_f = sb(p2, "ones_f", [P, P])
            junk = sb(p2, "junk", [P, NCAND, 2 * P], BF16)
            cnt = sb(p2, "cnt", [P, NCAND])
            offsets = sb(p2, "offsets", [P, len(SHIFTS), NCAND], I32)
            steps_of = sb(p2, "steps_of", [P, NCAND], I32)
            thr = sb(p2, "thr", [P, 1], I32)
            cand = sb(p2, "cand", [P, NCAND], I32)
            okc = sb(p2, "okc", [P, NCAND])
            thr_d = sb(p2, "thr_d", [P, E])
            thr_b = sb(p2, "thr_b", [P, E])
            marks = sb(p2, "marks", [P, NT, 2, E], BF16)
            above = sb(p2, "above", [P, E])
            slot_f = sb(p2, "slot_f", [P, NT, E])
            slot_e = sb(p2, "slot_e", [P, NT, E])
            slot_i = sb(p2, "slot_i", [P, NT, E], I32)
            sa = sb(p2, "sa", [P, NT, E], I32)
            sbb = sb(p2, "sbb", [P, NT, E], I32)
            sa_h = sb(p2, "sa_h", [P, NT * E], F16)
            sb_h = sb(p2, "sb_h", [P, NT * E], F16)
            tok = sb(p2, "tok", [P, NT * E], F16)
            hot_a = sb(p2, "hot_a", [P, NT * E, A_N], F16)
            hot_b = sb(p2, "hot_b", [P, B_N, NT * E], F16)

            def dve(waits, run):
                return put("dve", waits, run, s_sel)

            def pool(waits, run):
                return put("pool", waits, run, s_c2)

            t = pool(t_part1, lambda e: e.iota(tok[:, :].rearrange("p (t e) -> p t e", e=E), pattern=[[P, NT], [0, E]], base=-TOK0,
                                               channel_multiplier=1, allow_small_or_imprecise_dtypes=True))
            t_steps = pool([t], lambda e: e.iota(steps_of[:, :], pattern=[[1, NCAND]], base=0, channel_multiplier=0))
            pool([t], lambda e: e.memset(ones_f[:, :], 1.0))
            t = pool([t], lambda e: e.memset(ones_h[:, :], 1.0))
            t_c2 = pool([t], lambda e: e.affine_select(out=tri[:, :], in_=ones_h[:, :], compare_op=ALU.is_ge, fill=0.0,
                                                       base=0, pattern=[[1, P]], channel_multiplier=-1))
            t = dve(t_part1, lambda e: e.reduce_max(expert_of[:, :], ident[:, :].rearrange("p (t e) -> p e t", e=E), AX.X))
            t_same = dve([t], lambda e: e.tensor_copy(
                same[:, :].rearrange("p (t e) -> p t e", e=E),
                expert_of[:, :].rearrange("p (a e) -> p a e", a=1).to_broadcast([P, P // E, E])))
            dve([], lambda e: e.memset(thr[:, :], 0))
            dve([], lambda e: e.memset(cnt[:, :], float(K)))
            for k, shift in enumerate(SHIFTS):
                t_thr = dve([t_steps], lambda e, k=k, shift=shift: e.tensor_single_scalar(
                    offsets[:, k, :], steps_of[:, :], shift, ALU.logical_shift_left))

            split_early(0)
            split_early(1)

            bank, free = take_bank()

            def run(e):
                for r in range(2):
                    last = e.transpose(ps_gen[bank][:, r * P:(r + 1) * P],
                                       probs[:, r * 16:(r + 1) * 16, :].rearrange("p t e -> p (t e)"), ident[:, :])
                return last
            t = put("pe", free + t_part1, run, s_gen)
            t_pT = dve([t], lambda e: e.tensor_copy(pT[:, :], ps_gen[bank][:, 0:2 * P]))

            for k, shift in enumerate(SHIFTS):
                t = dve([t_thr], lambda e, k=k: e.tensor_tensor(
                    cand[:, :], offsets[:, k, :], thr[:, :].to_broadcast([P, NCAND]), ALU.bitwise_or))
                for j in range(1, NCAND):
                    t_n = dve([t, t_pT], lambda e, j=j: e.tensor_scalar(
                        junk[:, j, :], pT[:, :], cand[:, j:j + 1].bitcast(F32), 0.0, ALU.is_ge, ALU.add, accum_out=cnt[:, j:j + 1]))
                t = put("pe", [t_n, t_same], lambda e: e.matmul(ps_den[:, 0:NCAND], lhsT=same[:, :], rhs=cnt[:, :], start=True, stop=True), s_cnt)
                t = dve([t], lambda e: e.scalar_tensor_tensor(
                    okc[:, :], ps_den[:, 0:NCAND], float(K), cand[:, :].bitcast(F32), ALU.is_ge, ALU.mult))
                t_thr = dve([t], lambda e: e.reduce_max(thr[:, :].bitcast(F32), okc[:, :], AX.X))

            t = dve([t_thr], lambda e: e.tensor_scalar(thr_d[:, :], ident[:, 0:E], thr[:, 0:1].bitcast(F32), None, ALU.mult))
            t = put("pe", [t, t_c2], lambda e: e.matmul(ps_den[:, 0:E], lhsT=ones_f[:, :], rhs=thr_d[:, :], start=True, stop=True), s_cnt)
            t = dve([t], lambda e: e.tensor_copy(thr_b[:, :], ps_den[:, 0:E]))
            wide_thr = thr_b[:, :].rearrange("p (a e) -> p a e", a=1).to_broadcast([P, NT, E])
            dve([t], lambda e: e.tensor_tensor(marks[:, :, 0, :], probs[:, :, :], wide_thr, ALU.is_gt))
            t_marks = dve([], lambda e: e.tensor_tensor(marks[:, :, 1, :], probs[:, :, :], wide_thr, ALU.is_equal))

            def run(e):
                for n in range(NT):
                    last = e.matmul(ps_den[:, 0:E], lhsT=ones_h[:, :], rhs=marks[:, n, 0, :], start=(n == 0), stop=(n == NT - 1))
                return last
            t_above = put("pe", [t_marks, t_c2], run, s_tot2)

            def run(e):
                e.matmul(ps_att[:, :], lhsT=tri[:, :], rhs=marks[:, :, :, :].rearrange("p t m e -> p (t m e)"), start=True, stop=False)
                for n in range(NT - 1):
                    last = e.matmul(ps_att[:, (n + 1) * 2 * E:], lhsT=ones_h[:, :],
                                    rhs=marks[:, n:n + 1, :, :].rearrange("p t m e -> p t (m e)").to_broadcast([P, NT - 1 - n, 2 * E]),
                                    start=False, stop=(n == NT - 2))
                return last
            t_rank = put("pe", [], run, s_tot2)
            rank = ps_att[:, :].rearrange("p (t m e) -> p t m e", m=2, e=E)
            t = dve([t_above], lambda e: e.tensor_copy(above[:, :], ps_den[:, 0:E]))
            wide_above = above[:, :].rearrange("p (a e) -> p a e", a=1).to_broadcast([P, NT, E])
            t_e = dve([t, t_rank], lambda e: e.tensor_tensor(slot_e[:, :, :], rank[:, :, 1, :], wide_above, ALU.add))
            t_f = dve([], lambda e: e.tensor_tensor(slot_f[:, :, :], rank[:, :, 0, :], marks[:, :, 0, :], ALU.mult))
            t = dve([t_e], lambda e: e.tensor_tensor(slot_e[:, :, :], slot_e[:, :, :], marks[:, :, 1, :], ALU.mult))
            t = dve([t, t_f], lambda e: e.scalar_tensor_tensor(slot_i[:, :, :], slot_f[:, :, :], -1.0, slot_e[:, :, :], ALU.add, ALU.add))
            t_a = dve([t], lambda e: e.tensor_single_scalar(sa[:, :, :], slot_i[:, :, :], A_N - 1, ALU.bitwise_and))
            t_b = dve([], lambda e: e.tensor_single_scalar(sbb[:, :, :], slot_i[:, :, :], 5, ALU.arith_shift_right))
            t_a = dve([t_a], lambda e: e.tensor_copy(sa_h[:, :], sa[:, :, :].rearrange("p t e -> p (t e)")))
            t_b = dve([t_b], lambda e: e.tensor_copy(sb_h[:, :], sbb[:, :, :].rearrange("p t e -> p (t e)")))
            for a in range(A_N):
                dve([t_a], lambda e, a=a: e.tensor_single_scalar(hot_a[:, :, a], sa_h[:, :], float(a), ALU.is_equal))
            for n in range(B_N):
                t_hot = dve([t_b, t_c2], lambda e, n=n: e.scalar_tensor_tensor(
                    hot_b[:, n, :], sb_h[:, :], float(n), tok[:, :], ALU.is_equal, ALU.mult))
            t_idx = {}
            for hf in range(2):
                psum = ps_gen[hf]

                def run(e, hf=hf, psum=psum):
                    for n in range(NT):
                        c = slice(n * E + hf * HALF, n * E + (hf + 1) * HALF)
                        last = e.matmul(psum[:, 0:HALF * B_N], lhsT=hot_a[:, c, :].rearrange("p e a -> p (e a)"),
                                        rhs=hot_b[:, :, c].rearrange("p b e -> p e b"), start=(n == 0), stop=(n == NT - 1))
                    return last
                t = put("pe", [t_hot, t_pT], run, s_cnt)
                for e4 in range(HALF):
                    for r in range(P // QUAD):
                        srcv = psum[e4 * QUAD:(e4 + 1) * QUAD, e4 * B_N + r:(e4 + 1) * B_N:P // QUAD]
                        k = hf * HALF + e4
                        t_idx[k] = dve([t], lambda e, srcv=srcv, r=r, k=k: e.tensor_scalar(
                            idx[r * QUAD:(r + 1) * QUAD, k, :], srcv, float(TOK0), None, ALU.add))
            t_part2 = [t_idx[E - 1], (s_cnt, s_cnt.count), (s_tot2, s_tot2.count), t_c2]
            p2.close()

            hT = [[sb(p3, f"hT_{k}{i}", [P, DC, K], F32R) for k in ("hi", "lo")] for i in range(2)]
            gel = [sb(p3, f"gel{i}", [P, K]) for i in range(2)]
            gel_s = [[sb(p3, f"gel_{k}{i}", [P, K], F32R) for k in ("hi", "lo")] for i in range(2)]
            b2_b = [sb(p3, f"b2_b{i}", [P, D]) for i in range(2)]
            y_sb = [sb(p3, f"y_sb{i}", [P, D]) for i in range(TT)]
            y_out = [sb(p3, f"y_out{i}", [P, D]) for i in range(TT)]

            s_b1, s_b2 = sem("s_b1"), [sem(f"s_b2{i}") for i in range(2)]
            s_rows = [sem(f"s_rows{i}") for i in range(2 * TT)]
            s_up, s_gelu, s_gel_lo, s_down = sem("s_up"), sem("s_gelu"), sem("s_gel_lo"), sem("s_down")
            s_yb, s_y, s_add = sem("s_yb"), sem("s_y"), [sem(f"s_add{i}") for i in range(TT)]
            ps_up = ps_gen
            ps_y = [p[:, :] for p in ps_gen[2:2 + TT]]
            ps_tr = [ps_att, ps_den]
            up_free, tr_free = [[], []], [[], []]
            y_free = [[] for _ in range(TT)]

            t_b1in = put("sp", t_part1, lambda e: e.dma_start(b1_raw[:, :], b1.rearrange("e (j p) -> (e j) p", p=P)), s_b1, 16)
            t = put("pe", [t_b1in] + t_part2, lambda e: e.transpose(ps_att[:, 0:P], b1_raw[:, :], ident[:, :]), s_gen)
            t_b1 = put("dve", [t], lambda e: e.tensor_copy(b1_cols[:, :], ps_att[:, 0:P]), s_ev_dve)
            tr_free[0] = [t_b1]

            rows_free = [[] for _ in range(2 * TT)]
            t_rows = {}

            def gather(ex):
                for tt in range(TT):
                    slot = (ex % 2) * TT + tt
                    t_rows[ex, tt] = put("pool", rows_free[slot] + [t_idx[ex]] + t_hn_all, lambda e, slot=slot, tt=tt: e.indirect_dma_start(
                        rows[slot][:, :], None, hn_rows[:, :], bass.IndirectOffsetOnAxis(ap=idx[:, ex, tt:tt + 1], axis=0)), s_rows[slot], 16)

            hT_free = [[], []]
            t_hT = {}

            def transpose_rows(ex, tt):
                slot = (ex % 2) * TT + tt
                k = tt % 2
                psum = ps_tr[k]

                def run(e):
                    for c in range(DC):
                        last = e.transpose(psum[:, c * P:(c + 1) * P], rows[slot][:, c * P:(c + 1) * P], ident[:, :])
                    return last
                tf = put("pe", tr_free[k] + [t_rows[ex, tt]] + t_part2, run, s_gen)
                view = psum[:, :].rearrange("p (c t) -> p c t", c=DC)
                dst = [d[:, :, tt * P:(tt + 1) * P] for d in hT[ex % 2]]
                th = put("act", [tf] + hT_free[ex % 2], lambda e: e.activation(dst[0], view, ACT.Copy), s_ev_act)
                tl = put("dve", [tf, th] + hT_free[ex % 2], lambda e: e.tensor_tensor(dst[1], view, raw(dst[0]), ALU.subtract), s_ev_dve)
                tr_free[k] = [th, tl]
                t_hT[ex] = [th, tl]

            s_gfree = [[], []]
            t_gel = {}

            def up(ex, j):
                n = ex * NPIECE + j // 2
                w = w1s[n % NS]
                col = slice((j % 2) * P, (j % 2 + 1) * P)
                k = j % 2
                hh = hT[ex % 2]
                tf = put("pe", up_free[k] + [t_sp[n][0]] + t_hT[ex], lambda e: three(
                    ps_up[k][:, :], [((w[0][:, c, col], w[1][:, c, col]), (hh[0][:, c, :], hh[1][:, c, :])) for c in range(DC)], e), s_up)
                if j % 2:
                    split_free[n % NS][0] = [tf]
                if j == NF - 1:
                    hT_free[ex % 2] = [tf]
                bias = b1_cols[:, ex * NF + j:ex * NF + j + 1]
                tg = put("act", [tf, t_b1] + s_gfree[k], lambda e: e.activation(
                    gel[k][:, :], ps_up[k][:, :], ACT.Gelu_apprx_tanh, bias=bias), s_gelu)
                th = put("act", [tf, t_b1] + s_gfree[k], lambda e: e.activation(
                    gel_s[k][0][:, :], ps_up[k][:, :], ACT.Gelu_apprx_tanh, bias=bias), s_gelu)
                up_free[k] = [th]
                tl = put("dve", [th], lambda e: e.tensor_tensor(
                    gel_s[k][1][:, :], gel[k][:, :], raw(gel_s[k][0][:, :]), ALU.subtract), s_gel_lo)
                t_gel[ex, j] = [th, tl]

            def down(ex, j):
                n = ex * NPIECE + j // 2
                w = w2s[n % NS]
                k = j % 2

                def run(e, tiles=range(TT)):
                    for tt in tiles:
                        c = slice(tt * P, (tt + 1) * P)
                        gh, gl = gel_s[k][0][:, c], gel_s[k][1][:, c]
                        wh, wl = w[0][:, j % 2, :], w[1][:, j % 2, :]
                        e.matmul(ps_y[tt], lhsT=gh, rhs=wh, start=(j == 0), stop=False)
                        e.matmul(ps_y[tt], lhsT=gh, rhs=wl, start=False, stop=False)
                        last = e.matmul(ps_y[tt], lhsT=gl, rhs=wh, start=False, stop=(j == NF - 1))
                    return last
                groups = [[tt] for tt in range(TT)] if j in (0, NF - 1) else [range(TT)]
                tf = [put("pe", (y_free[g[0]] if j == 0 else []) + t_gel[ex, j] + [t_sp[n][1]],
                          lambda e, g=g: run(e, g), s_down) for g in groups]
                done, tf = tf, tf[-1]
                s_gfree[k] = [tf]
                if j % 2:
                    split_free[n % NS][1] = [tf]
                return done

            b2_free = [[], []]
            y_sb_free = [[] for _ in range(TT)]
            y_out_free = [[] for _ in range(TT)]
            t_b2 = {}

            def load_b2(ex):
                k = ex % 2
                t_b2[ex] = put("sp", b2_free[k] + t_part2 + t_part1, lambda e: e.dma_start(
                    b2_b[k][:, :], b2[ex:ex + 1, :].to_broadcast([P, D])), s_b2[k], 16)

            t_added = [list(t_x1_all)]

            def finish(ex, tf):
                k = ex % 2
                before = t_added[0]
                mine = []
                for tt in range(TT):
                    slot = k * TT + tt
                    ty = put("dve", [tf[tt], t_b2[ex]] + y_sb_free[tt], lambda e, tt=tt: e.tensor_tensor(
                        y_sb[tt][:, :], ps_y[tt], b2_b[k][:, :], ALU.add), s_yb)
                    y_free[tt] = [ty]
                    to = put("act", [ty] + y_out_free[tt], lambda e, tt=tt, slot=slot: e.activation(
                        y_out[tt][:, :], y_sb[tt][:, :], ACT.Copy, scale=rows[slot][:, D + ex:D + ex + 1]), s_y)
                    y_sb_free[tt] = [to]
                    rows_free[slot] = [to]
                    ta = put("pool", [to] + before, lambda e, tt=tt: e.indirect_dma_start(
                        out_tok, bass.IndirectOffsetOnAxis(ap=idx[:, ex, tt:tt + 1], axis=0),
                        y_out[tt][:, :], None, compute_op=ALU.add), s_add[tt], 16)
                    y_out_free[tt] = [ta]
                    mine.append(ta)
                b2_free[k] = [ty]
                t_added[0] = mine

            gather(0)
            load_b2(0)
            for tt in range(TT):
                transpose_rows(0, tt)
            gather(1)
            load_b2(1)
            order = [(ex, j) for ex in range(E) for j in range(NF)]
            up(0, 0)
            for i, (ex, j) in enumerate(order):
                if i + 1 < len(order):
                    up(*order[i + 1])
                tf = down(ex, j)
                if j == NF - 1:
                    finish(ex, tf)
                if j % 2 == 1:
                    n = i // 2
                    if n + NR < len(pieces):
                        load_piece(n + NR)
                    if n + 2 < len(pieces):
                        split_piece(n + 2)
                if ex + 1 < E and NF - 6 <= j < NF - 2:
                    transpose_rows(ex + 1, j - (NF - 6))
                if j == NF - 1 and ex + 2 < E:
                    gather(ex + 2)
                    load_b2(ex + 2)
            q.steps["pool"].append((t_added[0], lambda e: None, None, 0))

        with nc.Block() as block:
            @block.sync
            def _(e):
                q.emit("sp", e)

            @block.gpsimd
            def _(e):
                q.emit("pool", e)

            @block.scalar
            def _(e):
                q.emit("act", e)

            @block.vector
            def _(e):
                q.emit("dve", e)

            @block.tensor
            def _(e):
                q.emit("pe", e)


_INS = ['x', 'ctx_1024', 'mask_BxS2_bf1', 'L0_xattn_Wq', 'L0_xattn_bq', 'L0_xattn_Wk', 'L0_xattn_bk', 'L0_xattn_Wv',
        'L0_xattn_bv', 'L0_xattn_Wo', 'L0_xattn_bo', 'L0_ffn_Ws', 'L0_ffn_bs', 'L0_ffn_W1', 'L0_ffn_b1', 'L0_ffn_W2',
        'L0_ffn_b2']


def kernel(**inputs):
    import numpy as np
    import concourse.bacc as bacc
    from concourse.bass_utils import run_bass_kernel_spmd

    nc = bacc.Bacc("TRN2", target_bir_lowering=False, num_devices=1)
    arrays, args = {}, []
    for name in _INS:
        a = np.ascontiguousarray(inputs[name])
        arrays[f"in_{name}"] = a
        args.append(nc.dram_tensor(f"in_{name}", a.shape, mybir.dt.from_np(a.dtype), kind="ExternalInput").ap())
    b, s, d = inputs['x'].shape
    e = inputs['L0_ffn_Ws'].shape[1]
    out = nc.dram_tensor("out_x", (b, s, d), F32, kind="ExternalOutput").ap()
    hn_rows = nc.dram_tensor("hn_rows", (b * s, d + e), F32, kind="Internal").ap()
    mask_rows = nc.dram_tensor("mask_rows", inputs['mask_BxS2_bf1'].shape, F32R, kind="Internal").ap()
    attention_moe_kernel(nc, *args, out, hn_rows, mask_rows)
    r = run_bass_kernel_spmd(nc, [arrays], core_ids=[0])
    return r.results[0]["out_x"]
```
